# Optimizing a Trainium2 kernel written in Bass

```python
import numpy as np
import jax
import jax.numpy as jnp

def _softmax(x, axis=-1):
    return jax.nn.softmax(x, axis=axis)

def _gelu(x):
    return jax.nn.gelu(x, approximate=True)

def _silu(x):
    return jax.nn.silu(x)

def _sigmoid(x):
    return jax.nn.sigmoid(x)

def _layernorm(x, axis=-1, eps=1e-05):
    m = jnp.mean(x, axis=axis, keepdims=True)
    v = jnp.var(x, axis=axis, keepdims=True)
    return (x - m) / jnp.sqrt(v + eps)

def _scatter_add(tgt, idx, src, axis=0):
    return tgt.at[idx].add(src)

def _segment_sum(src, seg, n):
    return jax.ops.segment_sum(src, seg, n)
kernel_name = 'mk_seq_postln_d1_jaxref_r8_5652fb'

def setup_inputs(seed: int=0):
    np.random.seed(seed)
    _w = jnp.asarray

    def _L0_attn_setup():
        import jax, jax.numpy as jnp
        import numpy as np
        D_MODEL = 128
        N_HEADS = 16
        HEAD_DIM = D_MODEL // N_HEADS
        D_LATENT = 32
        LAMBDA_DECAY = 0.01
        TIME_STEP = 0.01
        CLAMP = 10000.0

        def _reference_tuple_inner(x, Wq, Wk, Wv, Wo, W_down_kv, W_up_k, W_up_v):
            B, S, _ = x.shape
            q = x @ Wq
            k = x @ Wk
            v = x @ Wv
            latent_kv = (k + v) @ W_down_kv
            k_rec = latent_kv @ W_up_k
            v_rec = latent_kv @ W_up_v

            def heads(t):
                return t.reshape(B, S, N_HEADS, HEAD_DIM).transpose(0, 2, 1, 3)
            qh, kh, vh = (heads(q), heads(k_rec), heads(v_rec))
            scale = 1.0 / (jnp.sqrt(jnp.float32(D_MODEL)) + 1e-08)
            scores = jnp.einsum('bhqd,bhkd->bhqk', qh, kh) * scale
            scores = jnp.clip(jnp.nan_to_num(scores, nan=-1000000000.0), -CLAMP, CLAMP)
            idx = jnp.arange(S, dtype=jnp.float32)
            decay = jnp.exp(-LAMBDA_DECAY * TIME_STEP * jnp.abs(idx[:, None] - idx[None, :]))
            scores = scores * decay[None, None, :, :]
            scores = jnp.clip(jnp.nan_to_num(scores, nan=-1000000000.0), -CLAMP, CLAMP)
            attn = jax.nn.softmax(scores, axis=-1)
            out = jnp.einsum('bhqk,bhkd->bhqd', attn, vh)
            out = out.transpose(0, 2, 1, 3).reshape(B, S, D_MODEL)
            return (out @ Wo, latent_kv)
        key = jax.random.key(seed)
        ks = jax.random.split(key, 8)
        B, S = (2, 256)

        def w(k, i, o):
            return jax.random.normal(k, (i, o), dtype=jnp.float32) * 0.02
        return {'x': jax.random.normal(ks[0], (B, S, D_MODEL), dtype=jnp.float32), 'Wq': w(ks[1], D_MODEL, D_MODEL), 'Wk': w(ks[2], D_MODEL, D_MODEL), 'Wv': w(ks[3], D_MODEL, D_MODEL), 'Wo': w(ks[4], D_MODEL, D_MODEL), 'W_down_kv': w(ks[5], D_MODEL, D_LATENT), 'W_up_k': w(ks[6], D_LATENT, D_MODEL), 'W_up_v': w(ks[7], D_LATENT, D_MODEL)}
    _L0_attn_in = _L0_attn_setup()

    def _L0_ffn_setup():
        import jax, jax.numpy as jnp
        import numpy as np
        E = 8
        TOPK = 2
        H = 128
        I = 128
        ISH = I * 2
        B, S = (2, 128)
        key = jax.random.key(seed)
        ks = jax.random.split(key, 7)
        s = 0.02
        return {'hidden_states': jax.random.normal(ks[0], (B, S, H), jnp.float32), 'w_router': jax.random.normal(ks[1], (H, E), jnp.float32) * s, 'fc1_w': jax.random.normal(ks[2], (E, H, 2 * I), jnp.float32) * s, 'fc2_w': jax.random.normal(ks[3], (E, I, H), jnp.float32) * s, 'gate_w': jax.random.normal(ks[4], (H, ISH), jnp.float32) * s, 'up_w': jax.random.normal(ks[5], (H, ISH), jnp.float32) * s, 'down_w': jax.random.normal(ks[6], (ISH, H), jnp.float32) * s}
    _L0_ffn_in = _L0_ffn_setup()
    _d = {'L0_attn_x': _L0_attn_in['x'], 'L0_attn_Wq': _L0_attn_in['Wq'], 'L0_attn_Wk': _L0_attn_in['Wk'], 'L0_attn_Wv': _L0_attn_in['Wv'], 'L0_attn_Wo': _L0_attn_in['Wo'], 'L0_attn_W_down_kv': _L0_attn_in['W_down_kv'], 'L0_attn_W_up_k': _L0_attn_in['W_up_k'], 'L0_attn_W_up_v': _L0_attn_in['W_up_v'], 'L0_ffn_w_router': _L0_ffn_in['w_router'], 'L0_ffn_fc1_w': _L0_ffn_in['fc1_w'], 'L0_ffn_fc2_w': _L0_ffn_in['fc2_w'], 'L0_ffn_gate_w': _L0_ffn_in['gate_w'], 'L0_ffn_up_w': _L0_ffn_in['up_w'], 'L0_ffn_down_w': _L0_ffn_in['down_w']}
    _x0 = _d['L0_attn_x']
    _d['L0_attn_x'] = jax.random.normal(jax.random.fold_in(jax.random.key(seed), 1), (4, 1024, 128), dtype=_x0.dtype)
    del _x0
    return _d

def reference(L0_attn_x, L0_attn_Wq, L0_attn_Wk, L0_attn_Wv, L0_attn_Wo, L0_attn_W_down_kv, L0_attn_W_up_k, L0_attn_W_up_v, L0_ffn_w_router, L0_ffn_fc1_w, L0_ffn_fc2_w, L0_ffn_gate_w, L0_ffn_up_w, L0_ffn_down_w):

    def _L0_attn_ref(x, Wq, Wk, Wv, Wo, W_down_kv, W_up_k, W_up_v):
        import jax, jax.numpy as jnp
        import numpy as np
        D_MODEL = 128
        N_HEADS = 16
        HEAD_DIM = D_MODEL // N_HEADS
        D_LATENT = 32
        LAMBDA_DECAY = 0.01
        TIME_STEP = 0.01
        CLAMP = 10000.0

        def _reference_tuple_inner(x, Wq, Wk, Wv, Wo, W_down_kv, W_up_k, W_up_v):
            B, S, _ = x.shape
            q = x @ Wq
            k = x @ Wk
            v = x @ Wv
            latent_kv = (k + v) @ W_down_kv
            k_rec = latent_kv @ W_up_k
            v_rec = latent_kv @ W_up_v

            def heads(t):
                return t.reshape(B, S, N_HEADS, HEAD_DIM).transpose(0, 2, 1, 3)
            qh, kh, vh = (heads(q), heads(k_rec), heads(v_rec))
            scale = 1.0 / (jnp.sqrt(jnp.float32(D_MODEL)) + 1e-08)
            scores = jnp.einsum('bhqd,bhkd->bhqk', qh, kh) * scale
            scores = jnp.clip(jnp.nan_to_num(scores, nan=-1000000000.0), -CLAMP, CLAMP)
            idx = jnp.arange(S, dtype=jnp.float32)
            decay = jnp.exp(-LAMBDA_DECAY * TIME_STEP * jnp.abs(idx[:, None] - idx[None, :]))
            scores = scores * decay[None, None, :, :]
            scores = jnp.clip(jnp.nan_to_num(scores, nan=-1000000000.0), -CLAMP, CLAMP)
            attn = jax.nn.softmax(scores, axis=-1)
            out = jnp.einsum('bhqk,bhkd->bhqd', attn, vh)
            out = out.transpose(0, 2, 1, 3).reshape(B, S, D_MODEL)
            return (out @ Wo, latent_kv)
        return _reference_tuple_inner(x, Wq, Wk, Wv, Wo, W_down_kv, W_up_k, W_up_v)[0]

    def _L0_ffn_ref(hidden_states, w_router, fc1_w, fc2_w, gate_w, up_w, down_w):
        import jax, jax.numpy as jnp
        import numpy as np
        E = 8
        TOPK = 2
        H = 128
        I = 128
        ISH = I * 2
        B, S = (2, 128)
        orig_shape = hidden_states.shape
        x = hidden_states.reshape(-1, orig_shape[-1])
        logits = x @ w_router
        top_logits, top_idx = jax.lax.top_k(logits, TOPK)
        scores = jax.nn.softmax(top_logits, axis=-1)
        flat_idx = top_idx.reshape(-1)
        sorted_idx = jnp.argsort(flat_idx)
        permuted = x[sorted_idx // TOPK]
        eid = flat_idx[sorted_idx]
        out_perm = jnp.zeros((permuted.shape[0], orig_shape[-1]), x.dtype)
        for e in range(E):
            m = (eid == e).astype(x.dtype)[:, None]
            h1 = permuted * m @ fc1_w[e]
            proj, gate = jnp.split(h1, 2, axis=-1)
            out_perm = out_perm + jax.nn.silu(proj) * gate @ fc2_w[e]
        unperm = jnp.zeros_like(out_perm).at[sorted_idx].set(out_perm)
        moe_out = (unperm.reshape(-1, TOPK, orig_shape[-1]) * scores[:, :, None]).sum(axis=1)
        moe_out = moe_out.reshape(orig_shape)
        shared = jax.nn.silu(hidden_states @ gate_w) * (hidden_states @ up_w) @ down_w
        return moe_out + shared
    x = L0_attn_x
    x = _layernorm(x + _L0_attn_ref(x, L0_attn_Wq, L0_attn_Wk, L0_attn_Wv, L0_attn_Wo, L0_attn_W_down_kv, L0_attn_W_up_k, L0_attn_W_up_v), axis=-1)
    x = _layernorm(x + _L0_ffn_ref(x, L0_ffn_w_router, L0_ffn_fc1_w, L0_ffn_fc2_w, L0_ffn_gate_w, L0_ffn_up_w, L0_ffn_down_w), axis=-1)
    return x

_drawn_inputs = setup_inputs


def setup_inputs(seed=0):
    import zlib

    import numpy as np

    out = dict(_drawn_inputs(seed))
    spreads = {}
    factors = {'L0_attn_Wq': 8.0,
     'L0_attn_Wk': 8.0,
     'L0_attn_Wv': 8.0,
     'L0_attn_Wo': 8.0,
     'L0_attn_W_down_kv': 8.0,
     'L0_attn_W_up_k': 8.0,
     'L0_attn_W_up_v': 8.0,
     'L0_ffn_w_router': 8.0,
     'L0_ffn_fc1_w': 8.0,
     'L0_ffn_fc2_w': 8.0,
     'L0_ffn_gate_w': 6.893,
     'L0_ffn_up_w': 6.851,
     'L0_ffn_down_w': 6.804}
    for name, (base, spread) in spreads.items():
        noise = np.random.default_rng([zlib.crc32(name.encode()), seed]).standard_normal(out[name].shape)
        drawn = base * np.exp(spread * noise) if base else spread * noise
        out[name] = jnp.asarray(drawn.astype(out[name].dtype))
    for name, factor in factors.items():
        out[name] = (out[name] * factor).astype(out[name].dtype)
    return out
```

```python
from contextlib import ExitStack

import numpy as np

import concourse.bass as bass
from concourse import mybir

F32 = mybir.dt.float32
BF16 = mybir.dt.bfloat16
I32 = mybir.dt.int32
U32 = mybir.dt.uint32
ALU = mybir.AluOpType
ACT = mybir.ActivationFunctionType
AX_X = mybir.AxisListType.X

P = 128
HEADS = 16
HD = 8
CLAMP = 10000.0
DECAY_RATE = 0.01 * 0.01
EPS = 1e-5
SCORE_LIMIT = 40.0
SUM_LIMIT = 1e16
NPART = 3
TERMS = NPART * NPART * HD


def shape_constants(S, D):
    pos = np.arange(S, dtype=np.float64) - S // 2
    rows = np.stack([np.exp(-DECAY_RATE * pos), np.exp(DECAY_RATE * pos)]).astype(np.float32)
    j, i = np.arange(P)[:, None].astype(np.float64), np.arange(P)[None, :].astype(np.float64)
    diag = np.exp(-2 * DECAY_RATE * np.maximum(j - i, 0.0))
    head_sum = np.zeros((P, 32))
    head_sum[np.arange(D), 2 * (np.arange(D) // (2 * HD)) + np.arange(D) % 2] = 1.0
    lane = np.tile(np.arange(8, dtype=np.float64), (P, 4))
    pack = np.concatenate([np.eye(P), diag, head_sum, lane, np.ones((P, 1))], axis=1).astype(np.float32)
    c = np.arange(2 * S - P, dtype=np.float64)[None, :]
    band = np.exp(-DECAY_RATE * np.abs(c - j - (S - P))).astype(np.float32)
    return rows, pack, band


def block_kernel(nc, x, Wq, Wk, Wv, Wo, Wd, Wuk, Wuv, Wr, fc1, fc2, gate_w, up_w, down_w,
                 decay_rows, const_pack, decay_band, out):
    B, S, D = x.shape
    L = Wd.shape[1]
    E, _, F2 = fc1.shape
    F = F2 // 2
    NT = S // P
    HALF = S // 2
    CT = HALF // P
    PAIRS = B * HEADS // 2
    PPB = HEADS // 2
    NCH = B * 2
    NE = E + gate_w.shape[1] // F
    SCALE = float(np.float32(1.0) / (np.sqrt(np.float32(D)) + np.float32(1e-8)))
    NORM_LIMIT = (SCORE_LIMIT / SCALE) ** 2
    assert D == P and HEADS * HD == P and F == P and S == 1024 and PPB == NT and NE == E + 2

    x_tiles = x.rearrange("b (t p) d -> b p t d", p=P)
    x_rows = x.rearrange("b s d -> (b s) d")
    out_rows = out.rearrange("b s d -> (b s) d")

    parts_dram = nc.dram_tensor("parts_dram", (2, NPART, B * P, 2 * S), BF16, kind="Internal").ap()
    raw_dram = nc.dram_tensor("raw_dram", (2, B * P, S), F32, kind="Internal").ap()

    with ExitStack() as ctx:
        def sb(name, shape, dt=F32):
            return ctx.enter_context(nc.sbuf_tensor(name, shape, dt))

        def sem(name):
            return ctx.enter_context(nc.semaphore(name))

        xT = sb("xT", [P, B * S])
        attn_pair = xT[:, :].rearrange("t (p g c d) -> t p g c d", p=PAIRS, g=4, c=CT)
        attn_chunk = xT[:, :].rearrange("t (b x h c d) -> t b h c x d", b=B, x=HEADS, h=2, c=CT)
        qT = sb("qT", [P, B * S])
        kT = sb("kT", [P, B * S])
        qkT = (qT, kT)
        V_all = sb("V_all", [P, PAIRS, NT, 2 * HD])
        stacks = sb("stacks", [P, 3 * 2 * 2 * 2 * S], BF16)
        sv = stacks[:, :].rearrange("r (u k h v s) -> r u k h v s", u=3, k=2, h=2, v=2)
        probs = sb("probs", [P, 6, S])
        stage = sb("stage", [P, 2, NPART, 2 * S], BF16)
        ptmp = sb("ptmp", [P, 2, S])
        rows_sb = sb("rows_sb", [P, 2, S])
        cpk = sb("cpk", [P, const_pack.shape[1]])
        Vring = sb("Vring", [P, 3, NT, 2, 32])
        osb = sb("osb", [P, HALF])
        rec = sb("rec", [P, 16])
        Wq_sb = sb("Wq_sb", [P, D])
        Wq_turned = sb("Wq_turned", [P, D])
        Wkv_sb = sb("Wkv_sb", [P, 3, D])
        Wd_sb = sb("Wd_sb", [P, L])
        Wu_sb = sb("Wu_sb", [L, 2, D])
        wfold = sb("wfold", [P, 4, D])
        sq = sb("sq", [P, 2, 2, HALF], BF16)
        head_sum_h = sb("head_sum_h", [P, 32], BF16)
        sqv = osb[:, :]
        sums = sb("sums", [P, 3 * NCH])
        nmax = sb("nmax", [64, NCH])
        test = sb("test", [P, 8])
        testv = sb("testv", [P, 3 * NCH])
        flag = sb("flag", [1, 1], I32)
        Wo_sb = sb("Wo_sb", [P, D])
        Wr_sb = sb("Wr_sb", [P, E])
        late = stage[:, :, :, :].rearrange("p k a s -> p (k a s)").bitcast(F32)
        up_sb = late[:, 0:NE * 2 * F].rearrange("p (e n) -> p e n", e=NE)
        dn_sb = late[:, NE * 2 * F:NE * (2 * F + D)].rearrange("p (e n) -> p e n", e=NE)
        small = sb("small", [P, 512])

        ident = cpk[:, 0:P]
        diag_fix = cpk[:, P:2 * P]
        head_sum = cpk[:, 2 * P:2 * P + 32]
        lane8 = cpk[:, 2 * P + 32:2 * P + 64]
        ones = cpk[:, 2 * P + 64:2 * P + 65]

        x_tok = probs[:, 0:B, :]
        gflat = stacks[:, :].bitcast(F32)
        g_qk = gflat[0:HD, 0:4 * S].rearrange("d (k h s) -> d k h s", k=2, h=2)
        g_band = gflat[:, 4 * S:4 * S + 2 * S - P]
        g_q = gflat[0:HD, 6 * S:6 * S + P]
        g_scores, g_probs, g_pT = probs[:, 0, :], probs[:, 1, :], probs[:, 2, :]
        g_stat = test[:, 4:8]
        NB = HALF
        ev = [gflat[:, n * NB:(n + 1) * NB] for n in range(22)]
        x_res = [ptmp[:, 0, q * NB:(q + 1) * NB] for q in range(2)]
        a_chunk = [ptmp[:, 1, q * NB:(q + 1) * NB] for q in range(2)]
        y_pre, xn, xnT, outb = (ev[2 * n:2 * n + 2] for n in range(4))
        silu, hid, part_e = (ev[12 + 2 * n:14 + 2 * n] for n in range(3))
        aT = ev[18:20]
        acc = ev[20:22]

        ps = ctx.enter_context(nc.psum_tensor("ps", [P, 8, HALF], F32))
        bank = [ps[:, n, :] for n in range(8)]
        slot = [ps[:, 2 * n:2 * n + 2, :].rearrange("p a b -> p (a b)") for n in range(3)]

        s_pack, s_rows, s_wkv, s_wq, s_late = (sem(n) for n in ("pack_loaded", "rows_loaded", "wkv_loaded", "wq_loaded", "late_loaded"))
        s_x = [sem(f"x_loaded{b}") for b in range(B)]
        wq_turned = sem("wq_turned")
        wkv_added, fold_done, fold_copied = sem("wkv_added"), sem("fold_done"), sem("fold_copied")
        xT_ready, xT_copied = sem("xT_ready"), sem("xT_copied")
        qk_ready, qk_kept = sem("qk_ready"), sem("qk_kept")
        v_ready, v_kept, v_squared = sem("v_ready"), sem("v_kept"), sem("v_squared")
        norm_ready, norm_maxed = sem("norm_ready"), sem("norm_maxed")
        prep_chain, stage_stored = sem("prep_chain"), sem("stage_stored")
        stage_ready = [sem("stage_ready_q"), sem("stage_ready_k")]
        test_ready, test_summed, flag_ready = sem("test_ready"), sem("test_summed"), sem("flag_ready")
        pad_zeroed = sem("pad_zeroed")
        pool_chain = sem("pool_chain")
        pool_stored = [sem("pool_stored_q"), sem("pool_stored_k")]
        pairs_stored = sem("pairs_stored")
        stack_loaded = [sem(f"stack_loaded{u}") for u in range(3)]

        scores_ready, diag_done = sem("scores_ready"), sem("diag_done")
        score_slots_free, prob_slots_free, exp_done = sem("score_slots_free"), sem("prob_slots_free"), sem("exp_done")
        v_copied, o_evacuated, o_turned, rec_done, o_kept = (sem(n) for n in ("v_copied", "o_evacuated", "o_turned", "rec_done", "o_kept"))
        g_raw, g_loaded, g_band_in, g_dve, g_pe, g_act = (sem(n) for n in ("g_raw", "g_loaded", "g_band_in", "g_dve", "g_pe", "g_act"))
        apart_ticks = sem("apart_ticks")
        attn_done = sem("attn_done")
        c_x = [sem("chunk_x0"), sem("chunk_x1")]
        c_a, c_aT, c_aTk, c_wo, c_y = (sem(n) for n in ("a_gathered", "a_turned", "a_kept", "wo_ready", "y_done"))
        c_lgk, pool_const, ln_chain, ln2_chain, route_chain = (sem(n) for n in ("logits_kept", "pool_const", "ln_chain", "ln2_chain", "route_chain"))
        c_var, c_rstd, c_xn, c_xnT, c_xnTk, c_lg = (sem(n) for n in ("var_done", "rstd_done", "xn_done", "xn_turned", "xn_kept", "logits_ready"))
        c_gap, c_exp, c_w = sem("gap_done"), sem("gap_exp"), sem("route_done")
        e_up, e_silu, e_hid, e_dn, e_part, e_acc = (sem(n) for n in ("up_ready", "silu_done", "hidden_done", "down_ready", "part_done", "acc_done"))
        c_shared, c_var2, c_rstd2, c_out = sem("shared_done"), sem("var2_done"), sem("rstd2_done"), sem("out_done")
        c_store = [sem("stored0"), sem("stored1")]

        block = ctx.enter_context(nc.Block())

        BODY_PAIRS = 3
        TPP = 2 * NT
        TPB = BODY_PAIRS * TPP
        ROUNDS = (PAIRS - 2) // BODY_PAIRS
        TAIL = ROUNDS * BODY_PAIRS
        FREE0 = 3
        LOADS = 2 * NPART * 16
        TILES = PAIRS * TPP
        G_LINKS = 9

        def apart(eng):
            eng.sem_inc(apart_ticks, 1)

        class Chain:

            def __init__(self, eng, s, per_call):
                self.eng, self.s, self.per_call = eng, s, per_call

            def start(self, call, offset=0):
                self.base, self.k = call * self.per_call + offset, 0

            def link(self, ins, wait=True):
                self.k += 1
                ins.then_inc(self.s, 1)
                if wait:
                    self.eng.wait_ge(self.s, self.base + self.k)

            def end(self):
                assert self.k == self.per_call, self.k

        at = [0]

        def small_tile(n, *dims):
            at[0] += n
            v = small[:, at[0] - n:at[0]]
            return v.rearrange("p (c k) -> p c k", c=CT) if dims else v

        stats = small_tile(CT * 6, 1)
        mv = small_tile(CT * 2, 1)
        stats2 = small_tile(CT * 6, 1)
        mv2 = small_tile(CT * 2, 1)
        var, rstd, var2, rstd2, gap, gexp, mhalf, ebase, w1, w2 = (small_tile(CT) for _ in range(10))
        logits, top8, idx_f, eq1, eq2 = (small_tile(CT * 8, 1) for _ in range(5))
        top_i = small_tile(CT * 8, 1).bitcast(U32)
        weights = [small_tile(CT * 8, 1) for _ in range(2)]

        @block.sync
        def _(sp):
            sp.dma_start(cpk[:, :], const_pack).then_inc(s_pack, 16)
            sp.dma_start(Wkv_sb[:, 0, :], Wk).then_inc(s_wkv, 16)
            sp.dma_start(Wkv_sb[:, 1, :], Wv).then_inc(s_wkv, 16)
            sp.dma_start(Wd_sb[:, :], Wd).then_inc(s_wkv, 16)
            sp.dma_start(Wu_sb[:, 0, :], Wuk).then_inc(s_wkv, 16)
            sp.dma_start(Wu_sb[:, 1, :], Wuv).then_inc(s_wkv, 16)
            sp.dma_start(Wq_sb[:, :], Wq).then_inc(s_wq, 16)
            for b in range(B):
                sp.dma_start(x_tok[:, b, :].rearrange("p (t d) -> p t d", t=NT), x_tiles[b]).then_inc(s_x[b], 16)
            for v in range(2):
                sp.dma_start(rows_sb[:, v, :], decay_rows[v:v + 1, :].to_broadcast([P, S])).then_inc(s_rows, 16)
            sp.dma_start(Wo_sb[:, :], Wo).then_inc(s_late, 16)
            sp.dma_start(Wr_sb[:, :], Wr).then_inc(s_late, 16)
            for n in range(2):
                sp.wait_ge(stage_ready[n], 1)
                sp.dma_start(parts_dram[n, :, 0:P, :].rearrange("a r s -> r a s"), stage[:, n, :, :]).then_inc(stage_stored, 16)

            def load_pair(p, u):
                here = bass.ds(p * 2 * HD, 2 * HD)
                for a in range(NPART):
                    rows = slice(a * NPART * HD, (a + 1) * NPART * HD)
                    q_part = parts_dram[0, a:a + 1, here, :].rearrange("a (d h) s -> a d (h s)", h=2)
                    k_parts = parts_dram[1, :, here, :].rearrange("b (d h) s -> b d (h s)", h=2)
                    for n, src in ((0, q_part.to_broadcast([NPART, HD, 4 * S])), (1, k_parts)):
                        dst = sv[rows, u, n, :, :, :].rearrange("r h v s -> r (h v s)")
                        sp.dma_start(dst, src).then_inc(stack_loaded[u], 16)

            sp.wait_ge(stage_stored, 32)
            sp.wait_ge(pad_zeroed, 3)
            for p in range(BODY_PAIRS):
                load_pair(p, p)

            sp.wait_ge(flag_ready, 1)
            fits = sp.value_load(flag[0:1, 0:1], min_val=0, max_val=P)
            with sp.If(fits >= P):
                with sp.Fori(1, ROUNDS) as i:
                    for u in range(BODY_PAIRS):
                        sp.wait_ge(scores_ready, i * TPB + (u - 2) * TPP)
                        apart(sp)
                        sp.wait_ge(pairs_stored, i * 3 + (u + 1))
                        load_pair(i * 3 + u, u)
                for p in range(TAIL, PAIRS):
                    sp.wait_ge(scores_ready, (p - 2) * TPP)
                    sp.wait_ge(pairs_stored, p + 1)
                    load_pair(p, p % 3)
                sp.wait_ge(pairs_stored, PAIRS)
            with sp.Else():
                for u in range(BODY_PAIRS):
                    sp.wait_ge(stack_loaded[u], LOADS)
                sp.wait_ge(qk_kept, 4 * B)
                sp.dma_start(g_band, decay_band).then_inc(g_band_in, 16)
                for n in range(2):
                    sp.dma_start(raw_dram[n].rearrange("(b r) s -> r b s", b=B),
                                 qkT[n][:, :].rearrange("r (b s) -> r b s", b=B)).then_inc(g_raw, 16)
                sp.wait_ge(g_raw, 32)
                with sp.Fori(0, PAIRS) as p:
                    sp.wait_ge(g_dve, p * (16 * G_LINKS) + 1)
                    for n in range(2):
                        sp.dma_start(g_qk[:, n, :, :],
                                     raw_dram[n, bass.ds(p * 2 * HD, 2 * HD), :].rearrange("(d h) s -> d h s", h=2)).then_inc(g_loaded, 16)

            sp.wait_ge(stage_stored, 32)
            sp.dma_start(up_sb[:, 0:E, :], fc1.rearrange("e h n -> h e n")).then_inc(s_late, 16)
            sp.dma_start(dn_sb[:, 0:E, :], fc2.rearrange("e i h -> i e h")).then_inc(s_late, 16)
            sp.dma_start(up_sb[:, E:NE, 0:F], gate_w.rearrange("h (j n) -> h j n", j=2)).then_inc(s_late, 16)
            sp.dma_start(up_sb[:, E:NE, F:2 * F], up_w.rearrange("h (j n) -> h j n", j=2)).then_inc(s_late, 16)
            sp.dma_start(dn_sb[:, E:NE, :], down_w.rearrange("(j i) h -> i j h", j=2)).then_inc(s_late, 16)

            def chunk_io(c, q, first):
                if not first:
                    sp.wait_ge(c_y, c - 1)
                sp.dma_start(x_res[q].rearrange("p (t d) -> p t d", t=CT),
                             x_rows[bass.ds(c * HALF, HALF), :].rearrange("(t p) d -> p t d", p=P)).then_inc(c_x[q], 16)

            def chunk_store(c, q):
                sp.wait_ge(c_out, c + 1)
                sp.dma_start(out_rows[bass.ds(c * HALF, HALF), :].rearrange("(t p) d -> p t d", p=P),
                             outb[q].rearrange("p (t d) -> p t d", t=CT)).then_inc(c_store[q], 16)

            for q in range(2):
                sp.sem_inc(c_store[q], 16)
            chunk_io(0, 0, True)
            chunk_io(1, 1, True)
            with sp.Fori(0, NCH // 2 - 1) as i:
                for q in range(2):
                    chunk_io(i * 2 + (q + 2), q, False)
                    chunk_store(i * 2 + q, q)
            for q in range(2):
                chunk_store(NCH - 2 + q, q)
            for q in range(2):
                sp.wait_ge(c_store[q], 16 * NCH // 2 + 16)


        @block.gpsimd
        def _(pool):
            def split(src, n, v, k0):
                tab = rows_sb[:, v ^ n, :]
                hi, mid, lo = (stage[:, n, a, v * S:(v + 1) * S] for a in range(NPART))
                f, r = ptmp[:, 0, :], ptmp[:, 1, :]
                nc.gpsimd.tensor_tensor(f, src, tab, ALU.mult).then_inc(pool_chain, 1)
                nc.gpsimd.tensor_tensor(hi, src, tab, ALU.mult).then_inc(pool_chain, 1)
                pool.wait_ge(pool_chain, k0 + 2)
                nc.gpsimd.tensor_tensor(r, f, hi, ALU.subtract).then_inc(pool_chain, 1)
                nc.gpsimd.tensor_tensor(mid, f, hi, ALU.subtract).then_inc(pool_chain, 1)
                pool.wait_ge(pool_chain, k0 + 4)
                nc.gpsimd.tensor_tensor(lo, r, mid, ALU.subtract).then_inc(pool_chain, 1)
                pool.wait_ge(pool_chain, k0 + 5)

            pool.wait_ge(s_wq, 16)
            for h in range(2):
                nc.gpsimd.tensor_copy(Wq_turned[:, :].rearrange("p (g d h) -> p h g d", g=PPB, h=2)[:, h],
                                      Wq_sb[:, :].rearrange("p (g h d) -> p h g d", g=PPB, h=2)[:, h]).then_inc(wq_turned, 1)
            pool.wait_ge(s_rows, 32)
            pool.wait_ge(qk_kept, 4)
            split(kT[:, 0:S], 1, 0, 0)
            split(kT[:, 0:S], 1, 1, 5)
            pool.sem_inc(stage_ready[1], 1)

            pool.wait_ge(flag_ready, 1)
            fits = pool.value_load(flag[0:1, 0:1], min_val=0, max_val=P)
            with pool.If(fits >= P):
                pool.wait_ge(stage_stored, 32)
                pool.sem_inc(pairs_stored, PPB)
                with pool.Fori(1, B) as b:
                    for n in range(2):
                        for v in range(2):
                            split(qkT[n][:, bass.ds(b * S, S)], n, v, b * 20 + (n * 10 + v * 5 - 10))
                            apart(pool)
                        pool.dma_start(parts_dram[n, :, bass.ds(b * P, P), :].rearrange("a r s -> r a s"),
                                       stage[:, n, :, :]).then_inc(pool_stored[n], 16)
                    for n in range(2):
                        pool.wait_ge(pool_stored[n], b * 16)
                    pool.sem_inc(pairs_stored, PPB)
                pool.wait_ge(o_kept, PPB)
            with pool.Else():
                pool.wait_ge(attn_done, 1)

            nc.gpsimd.memset(mhalf, -0.5).then_inc(pool_const, 1)
            nc.gpsimd.memset(ebase, float(np.e)).then_inc(pool_const, 1)
            pool.wait_ge(pool_const, 2)

            def gather(c, b, q):
                if b is not None:
                    pool.wait_ge(c_xnTk, c)
                nc.gpsimd.tensor_copy(a_chunk[q].rearrange("t (o c h d) -> t o c h d", o=1, c=CT, h=HEADS),
                                      attn_chunk[:, bass.ds(0 if b is None else b, 1), q, :, :, :]).then_inc(c_a, 1)

            def ln_power(c):
                pool.wait_ge(c_var, c + 1)
                nc.gpsimd.tensor_tensor(rstd, var, mhalf, ALU.pow).then_inc(c_rstd, 1)

            def step(c, b, q, last, previous=True):
                if not last:
                    gather(c + 1, b + q, 1 - q)
                if previous:
                    finish(c - 1)
                pool.wait_ge(c_gap, c + 1)
                nc.gpsimd.tensor_tensor(gexp, ebase, gap, ALU.pow).then_inc(c_exp, 1)
                for e in range(E):
                    pool.wait_ge(e_part, c * E + (e + 1))
                    if e:
                        pool.wait_ge(e_acc, c * E + e)
                    nc.gpsimd.tensor_tensor(acc[q], xn[q] if e == 0 else acc[q], part_e[e % 2], ALU.add).then_inc(e_acc, 1)
                    if e == 2 and not last:
                        ln_power(c + 1)

            def finish(c):
                pool.wait_ge(c_var2, c + 1)
                nc.gpsimd.tensor_tensor(rstd2, var2, mhalf, ALU.pow).then_inc(c_rstd2, 1)

            gather(0, None, 0)
            ln_power(0)
            step(0, 0, 0, False, previous=False)
            with pool.Fori(0, NCH // 2 - 1) as i:
                step(i * 2 + 1, i, 1, False)
                step(i * 2 + 2, i + 1, 0, False)
            step(NCH - 1, NCH // 2 - 1, 1, True)
            finish(NCH - 1)

        @block.scalar
        def _(act):
            def turned(ap, order):
                return [ap.rearrange(f"p ({order}) -> p h g d", g=PPB, h=2)[:, h] for h in range(2)]

            k_weight = list(zip(turned(wfold[:, 2, :], "g d h"), turned(bank[4][:, 0:P], "g h d")))
            for done, copies in ((1, [(wfold[:, 0, :], bank[2][:, 0:P])]), (2, [(wfold[0:L, 1, :], bank[3][0:L, 0:P])]),
                                 (3, k_weight), (4, [(wfold[:, 3, :], bank[5][:, 0:P])])):
                act.wait_ge(fold_done, done)
                for dst, src in copies:
                    nc.scalar.activation(dst, src, ACT.Copy).then_inc(fold_copied, 1)
            for b in range(B):
                for h in range(2):
                    act.wait_ge(xT_ready, 2 * b + h + 1)
                    nc.scalar.activation(xT[:, b * S + h * HALF:b * S + (h + 1) * HALF], bank[h], ACT.Copy).then_inc(xT_copied, 1)
                for h in range(2):
                    if b:
                        act.wait_ge(norm_ready, 2 * b + h - 1)
                    for n in range(2):
                        act.wait_ge(qk_ready, 4 * b + 2 * h + n + 1)
                        src = bank[2 + 2 * h + n]
                        nc.scalar.activation(qkT[n][:, b * S + h * HALF:b * S + (h + 1) * HALF], src, ACT.Copy)
                        k = n * NCH + 2 * b + h
                        nc.scalar.activation(sq[:, h, n, :], src, ACT.Square, accum_out=sums[:, k:k + 1]).then_inc(qk_kept, 1)
                for h in range(2):
                    act.wait_ge(v_kept, 2 * b + h + 1)
                    if b or h:
                        act.wait_ge(v_squared, 2 * b + h)
                    k = 2 * NCH + 2 * b + h
                    nc.scalar.activation(sqv.rearrange("p (w t e) -> p w t e", w=PPB, t=CT),
                                         V_all[:, b * PPB:(b + 1) * PPB, CT * h:CT * (h + 1), :], ACT.Square,
                                         accum_out=sums[:, k:k + 1]).then_inc(v_squared, 1)

            act.wait_ge(flag_ready, 1)
            fits = act.value_load(flag[0:1, 0:1], min_val=0, max_val=P)
            with act.If(fits >= P):
                with act.Fori(0, ROUNDS) as i:
                    for m in range(TPB):
                        if m % 2 == 0:
                            act.wait_ge(prob_slots_free, i * (TPB // 2) + (m // 2 + 1))
                        act.wait_ge(diag_done, i * TPB + (m + 1))
                        nc.scalar.activation(probs[:, m % 6, :], slot[m % 3], ACT.Exp, scale=SCALE).then_inc(score_slots_free, 1)
                for m in range(TAIL * TPP, TILES):
                    if m % 2 == 0:
                        act.wait_ge(prob_slots_free, m // 2 + 1)
                    act.wait_ge(diag_done, m + 1)
                    nc.scalar.activation(probs[:, m % 6, :], slot[m % 3], ACT.Exp, scale=SCALE).then_inc(score_slots_free, 1)
            with act.Else():
                with act.Fori(0, PAIRS * 2 * NT) as n:
                    act.wait_ge(g_dve, n * G_LINKS + 7)
                    nc.scalar.activation(g_probs, g_scores, ACT.Exp, bias=g_stat[:, 0:1],
                                         accum_out=g_stat[:, 1:2]).then_inc(g_act, 1)

            def keep_a(c, q):
                act.wait_ge(c_aT, c + 1)
                nc.scalar.activation(aT[q], bank[6], ACT.Copy).then_inc(c_aTk, 1)

            def keep_x(c, q):
                act.wait_ge(c_xnT, c + 1)
                nc.scalar.activation(xnT[q], bank[6], ACT.Copy).then_inc(c_xnTk, 1)

            def step(c, b, q, last):
                for e in range(NE):
                    act.wait_ge(e_up, c * NE + (e + 1))
                    nc.scalar.activation(silu[e % 2], bank[e % 2], ACT.Silu).then_inc(e_silu, 1)
                    if e == 2 and not last:
                        keep_a(c + 1, 1 - q)
                    if e == 7 and not last:
                        keep_x(c + 1, 1 - q)

            keep_a(0, 0)
            keep_x(0, 0)
            step(0, 0, 0, False)
            with act.Fori(0, NCH // 2 - 1) as i:
                step(i * 2 + 1, i, 1, False)
                step(i * 2 + 2, i + 1, 0, False)
            step(NCH - 1, NCH // 2 - 1, 1, True)

        @block.tensor
        def _(pe):
            mm = nc.tensor.matmul
            pe.wait_ge(s_pack, 16)
            pe.wait_ge(wkv_added, 1)
            nc.tensor.transpose(bank[2][:, 0:P], Wkv_sb[:, 2, :], ident).then_inc(fold_done, 1)
            pe.wait_ge(fold_copied, 1)
            mm(bank[3][0:L, 0:P], Wd_sb[:, :], wfold[:, 0, :], start=True, stop=True).then_inc(fold_done, 1)
            pe.wait_ge(fold_copied, 2)
            for n in range(2):
                mm(bank[4 + n][:, 0:P], wfold[0:L, 1, :], Wu_sb[:, n, :], start=True, stop=True).then_inc(fold_done, 1)
            pe.wait_ge(fold_copied, 5)
            pe.wait_ge(wq_turned, 2)
            for b in range(B):
                pe.wait_ge(s_x[b], 16)
                if b:
                    pe.wait_ge(xT_copied, 2 * b)
                for h in range(2):
                    for t in range(CT):
                        last = nc.tensor.transpose(bank[h][:, t * P:(t + 1) * P],
                                                   x_tok[:, b, (h * CT + t) * P:(h * CT + t + 1) * P], ident)
                    last.then_inc(xT_ready, 1)
                for h in range(2):
                    pe.wait_ge(xT_copied, 2 * b + h + 1)
                    if b:
                        pe.wait_ge(qk_kept, 4 * (b - 1) + 2 * h + 2)
                    rhs = xT[:, b * S + h * HALF:b * S + (h + 1) * HALF]
                    mm(bank[2 + 2 * h], Wq_turned[:, :], rhs, start=True, stop=True).then_inc(qk_ready, 1)
                    mm(bank[3 + 2 * h], wfold[:, 2, :], rhs, start=True, stop=True).then_inc(qk_ready, 1)
                for h in range(2):
                    if b or h:
                        pe.wait_ge(v_kept, 2 * b + h)
                    for t in range(CT):
                        k = b * S + (h * CT + t) * P
                        last = mm(bank[7][:, t * P:(t + 1) * P], xT[:, k:k + P], wfold[:, 3, :], start=True, stop=True)
                    last.then_inc(v_ready, 1)
                    pe.wait_ge(qk_kept, 4 * b + 2 * h + 2)
                    pe.wait_ge(norm_maxed, 2 * b + h + 1)
                    for n in range(2):
                        last = mm(bank[6][32 * n:32 * n + 32, :], head_sum_h[:, :], sq[:, h, n, :], start=True, stop=True)
                    last.then_inc(norm_ready, 1)
            pe.wait_ge(test_ready, 1)
            mm(bank[0][0:1, 0:1], test[:, 2:3], ones, start=True, stop=True).then_inc(test_summed, 1)

            pe.wait_ge(flag_ready, 1)
            fits = pe.value_load(flag[0:1, 0:1], min_val=0, max_val=P)
            with pe.If(fits >= P):
                def score_tile(i, m):
                    u, kt, h = (m // TPP) % BODY_PAIRS, (m % TPP) // 2, m % 2
                    if m % TPP == 0:
                        pe.wait_ge(stack_loaded[u], (i + m // TPB) * LOADS + LOADS)
                    pe.wait_ge(score_slots_free, i * TPB + (m + 1))
                    cuts = sorted({0, kt * P, HALF, S})
                    for lo, hi in zip(cuts, cuts[1:]):
                        v = 0 if lo >= kt * P else 1
                        last = mm(slot[m % 3][:, lo:hi], sv[:, u, 1, h, v, kt * P:(kt + 1) * P], sv[:, u, 0, h, v, lo:hi],
                                  start=True, stop=True)
                    last.then_inc(scores_ready, 1)

                def output_group(i, g):
                    u, kt = (g // NT) % BODY_PAIRS, g % NT
                    if kt == 0:
                        pe.wait_ge(v_copied, i * BODY_PAIRS + (g // NT + 1))
                        if g:
                            pe.wait_ge(o_evacuated, i * BODY_PAIRS + g // NT)
                    pe.wait_ge(score_slots_free, i * TPB + (2 * g + 2 + FREE0))
                    for h in range(2):
                        for qh in range(2):
                            r = 32 * (2 * h + qh)
                            last = mm(bank[6][r:r + 32, :], Vring[:, u, kt, h, :],
                                      probs[:, (2 * g + h) % 6, qh * HALF:(qh + 1) * HALF], start=(kt == 0), stop=(kt == NT - 1))
                    last.then_inc(prob_slots_free, 1)

                def turn_output(i, p):
                    pe.wait_ge(o_evacuated, i * BODY_PAIRS + (p + 1))
                    for c in range(CT):
                        last = nc.tensor.transpose(bank[7][:, c * P:(c + 1) * P], osb[:, c * P:(c + 1) * P], ident)
                    last.then_inc(o_turned, 1)

                def group_step(i, g, tiles_left=True):
                    if tiles_left or 2 * g + 4 < TILES:
                        score_tile(i, 2 * g + 4)
                    if g % NT == 0 and g:
                        turn_output(i, g // NT - 1)
                    output_group(i, g)
                    if tiles_left or 2 * g + 5 < TILES:
                        score_tile(i, 2 * g + 5)

                for m in range(4):
                    score_tile(0, m)
                group_step(0, 0)
                with pe.Fori(0, ROUNDS) as i:
                    for g in range(1, TPB // 2 + 1):
                        group_step(i, g)
                for g in range(TAIL * NT + 1, TILES // 2):
                    group_step(0, g, tiles_left=False)
                turn_output(0, PAIRS - 1)
            with pe.Else():
                with pe.Fori(0, PAIRS) as p:
                    for h in range(2):
                        with pe.Fori(0, NT) as t:
                            n = p * 16 + h * 8 + t
                            pe.wait_ge(g_dve, n * G_LINKS + 2)
                            for k in range(2):
                                last = mm(bank[k], g_q, g_qk[:, 1, h, k * HALF:(k + 1) * HALF], start=True, stop=True)
                            last.then_inc(g_pe, 1)
                            pe.wait_ge(g_act, n + 1)
                            for k in range(NT):
                                last = nc.tensor.transpose(slot[1][:, k * P:(k + 1) * P], g_probs[:, k * P:(k + 1) * P], ident)
                            last.then_inc(g_pe, 1)
                            pe.wait_ge(g_dve, n * G_LINKS + 8)
                            for k in range(NT):
                                last = mm(bank[4][:, 0:HD], g_pT[:, k * P:(k + 1) * P],
                                          V_all[:, bass.ds(p, 1), k, h * HD:(h + 1) * HD].rearrange("t o d -> t (o d)"),
                                          start=(k == 0), stop=(k == NT - 1))
                            last.then_inc(g_pe, 1)

            pe.wait_ge(s_late, 7 * 16)

            def turn_a(c, q, first=False):
                pe.wait_ge(c_a, c + 1)
                if not first:
                    pe.wait_ge(c_xnTk, c)
                for t in range(CT):
                    last = nc.tensor.transpose(bank[6][:, t * P:(t + 1) * P], a_chunk[q][:, t * P:(t + 1) * P], ident)
                last.then_inc(c_aT, 1)

            def project(c, q, first=False):
                pe.wait_ge(c_aTk, c + 1)
                if not first:
                    pe.wait_ge(c_lgk, c)
                for t in range(CT):
                    last = mm(bank[7][:, t * P:(t + 1) * P], aT[q][:, t * P:(t + 1) * P], Wo_sb[:, :], start=True, stop=True)
                last.then_inc(c_wo, 1)

            def turn_x(c, q):
                pe.wait_ge(c_xn, c + 1)
                for t in range(CT):
                    last = nc.tensor.transpose(bank[6][:, t * P:(t + 1) * P], xn[q][:, t * P:(t + 1) * P], ident)
                last.then_inc(c_xnT, 1)

            def route(c, q):
                pe.wait_ge(c_xnTk, c + 1)
                pe.wait_ge(c_y, c + 1)
                for t in range(CT):
                    last = mm(bank[7][:, t * E:(t + 1) * E], xnT[q][:, t * P:(t + 1) * P], Wr_sb[:, :], start=True, stop=True)
                last.then_inc(c_lg, 1)

            def up(c, q, e):
                pe.wait_ge(e_hid, c * NE + (e + 1))
                if e == 0:
                    pe.wait_ge(c_xnTk, c + 1)
                mm(bank[e % 2], up_sb[:, e, 0:F], xnT[q], start=True, stop=True)
                mm(bank[2 + e % 2], up_sb[:, e, F:2 * F], xnT[q], start=True, stop=True).then_inc(e_up, 1)

            def down(c, e):
                pe.wait_ge(e_hid, c * NE + (e + 3))
                if e == 0:
                    pe.wait_ge(c_shared, c + 1)
                elif e >= 2:
                    pe.wait_ge(e_part, c * E + (e - 1))
                for t in range(CT):
                    last = mm(bank[4 + e % 2][:, t * P:(t + 1) * P], hid[e % 2][:, t * P:(t + 1) * P], dn_sb[:, e, :], start=True, stop=True)
                last.then_inc(e_dn, 1)

            def down_shared(c):
                pe.wait_ge(e_hid, c * NE + (NE + 2))
                pe.wait_ge(e_part, c * E + (E - 1))
                for t in range(CT):
                    mm(bank[4][:, t * P:(t + 1) * P], hid[0][:, t * P:(t + 1) * P], dn_sb[:, E, :], start=True, stop=False)
                    last = mm(bank[4][:, t * P:(t + 1) * P], hid[1][:, t * P:(t + 1) * P], dn_sb[:, E + 1, :], start=False, stop=True)
                last.then_inc(e_dn, 1)

            def step(c, b, q, last):
                up(c, q, 0)
                for e in range(1, NE):
                    up(c, q, e)
                    if not last and e == 3:
                        project(c + 1, 1 - q)
                    if e < E:
                        down(c, e - 1)
                    if e == NE - 1:
                        down(c, E - 1)
                        if not last:
                            route(c + 1, 1 - q)
                    if not last:
                        if e == 1:
                            turn_a(c + 1, 1 - q)
                        if e == 6:
                            turn_x(c + 1, 1 - q)
                down_shared(c)

            turn_a(0, 0, first=True)
            pe.wait_ge(attn_done, 1)
            project(0, 0, first=True)
            turn_x(0, 0)
            route(0, 0)
            step(0, 0, 0, False)
            with pe.Fori(0, NCH // 2 - 1) as i:
                step(i * 2 + 1, i, 1, False)
                step(i * 2 + 2, i + 1, 0, False)
            step(NCH - 1, NCH // 2 - 1, 1, True)

        @block.vector
        def _(dve):
            tt, ts = nc.vector.tensor_tensor, nc.vector.tensor_scalar
            dve.wait_ge(s_wkv, 80)
            tt(Wkv_sb[:, 2, :], Wkv_sb[:, 0, :], Wkv_sb[:, 1, :], ALU.add).then_inc(wkv_added, 1)
            for u in range(3):
                nc.vector.memzero(sv[64:P, u].rearrange("r k h v s -> r (k h v s)").bitcast(F32)).then_inc(pad_zeroed, 1)
            nc.vector.memset(Vring[:, :, :, :, :], 0.0).then_inc(prep_chain, 1)
            nc.vector.memset(test[:, 0:1], 1.0).then_inc(prep_chain, 1)
            dve.wait_ge(s_pack, 16)
            nc.vector.tensor_copy(head_sum_h[:, :], head_sum).then_inc(norm_maxed, 1)
            dve.wait_ge(prep_chain, 1)
            nc.vector.memset(Vring[:, :, :, :, HD:HD + 1], 1.0).then_inc(prep_chain, 1)
            links = [3]

            def link(ins):
                links[0] += 1
                ins.then_inc(prep_chain, 1)
                dve.wait_ge(prep_chain, links[0])

            for b in range(B):
                for h in range(2):
                    dve.wait_ge(v_ready, 2 * b + h + 1)
                    nc.vector.tensor_copy(V_all[:, b * PPB:(b + 1) * PPB, CT * h:CT * (h + 1), :].rearrange("p w t e -> p t w e"),
                                          bank[7].rearrange("p (t w e) -> p t w e", t=CT, w=PPB)).then_inc(v_kept, 1)
                    dve.wait_ge(norm_ready, 2 * b + h + 1)
                    nc.vector.reduce_max(nmax[:, 2 * b + h:2 * b + h + 1], bank[6][0:64, :], AX_X).then_inc(norm_maxed, 1)
                if b < 2:
                    v = b
                    dve.wait_ge(qk_kept, 4)
                    dve.wait_ge(s_rows, 32)
                    hi, mid, lo = (stage[:, 0, a, v * S:(v + 1) * S] for a in range(NPART))
                    f, r = probs[:, 4, :], probs[:, 5, :]
                    link(tt(f, qT[:, 0:S], rows_sb[:, v, :], ALU.mult))
                    link(nc.vector.tensor_copy(hi, f))
                    link(tt(r, f, hi, ALU.subtract))
                    link(nc.vector.tensor_copy(mid, r))
                    link(tt(lo, r, mid, ALU.subtract))
                    if v == 1:
                        dve.sem_inc(stage_ready[0], 1)

            dve.wait_ge(norm_maxed, 2 * B + 1)
            link(nc.vector.reduce_max(testv[0:64, 0:1], nmax[:, :], AX_X))
            link(nc.vector.tensor_copy(testv[0:32, 1:2], testv[32:64, 0:1]))
            link(tt(testv[0:32, 2:3], testv[0:32, 0:1], testv[0:32, 1:2], ALU.mult))
            link(ts(test[0:32, 0:1], testv[0:32, 2:3], NORM_LIMIT, None, ALU.is_le))
            dve.wait_ge(v_squared, 2 * B)
            dve.wait_ge(qk_kept, 4 * B)
            link(ts(testv[:, :], sums[:, :], SUM_LIMIT, None, ALU.is_le))
            link(nc.vector.tensor_reduce(test[:, 1:2], testv[:, :], AX_X, ALU.min))
            tt(test[:, 2:3], test[:, 0:1], test[:, 1:2], ALU.mult).then_inc(test_ready, 1)
            dve.wait_ge(test_summed, 1)
            nc.vector.tensor_copy(flag[0:1, 0:1], bank[0][0:1, 0:1]).then_inc(flag_ready, 1)
            dve.wait_ge(flag_ready, 1)
            fits = dve.value_load(flag[0:1, 0:1], min_val=0, max_val=P)

            with dve.If(fits >= P):
                def copy_v(i, p):
                    nc.vector.tensor_copy(Vring[:, p % 3, :, :, 0:HD],
                                          V_all[:, bass.ds(i * BODY_PAIRS + p, 1), :, :].rearrange("r o t (h d) -> r (o t) h d", h=2)).then_inc(v_copied, 1)

                def fix_diagonal(i, m):
                    kt = (m % TPP) // 2
                    dve.wait_ge(scores_ready, i * TPB + (m + 1))
                    d = slot[m % 3][:, kt * P:(kt + 1) * P]
                    tt(d, d, diag_fix, ALU.mult).then_inc(diag_done, 1)

                def evacuate(i, p):
                    dve.wait_ge(prob_slots_free, (i * BODY_PAIRS + (p + 1)) * NT + FREE0)
                    nc.vector.tensor_copy(osb[:, :], bank[6]).then_inc(o_evacuated, 1)

                def normalise(i, p):
                    dve.wait_ge(o_turned, i * BODY_PAIRS + (p + 1))
                    o = bank[7].rearrange("t (c g r) -> t g c r", c=CT, g=4)
                    rv = rec[:, :].rearrange("t (g c) -> t g c", g=4)
                    nc.vector.reciprocal(rv, o[:, :, :, HD]).then_inc(rec_done, 1)
                    dve.wait_ge(rec_done, i * BODY_PAIRS + (p + 1))
                    tt(attn_pair[:, bass.ds(i * BODY_PAIRS + p, 1), :, :, :].rearrange("t o g c d -> t (o g c) d"),
                       o[:, :, :, 0:HD].rearrange("t g c d -> t g c d"),
                       rv.unsqueeze(3).to_broadcast([P, 4, CT, HD]), ALU.mult).then_inc(o_kept, 1)

                def tile_step(i, m, final=False):
                    r, p = m % TPP, m // TPP
                    if r == 3:
                        evacuate(i, p - 1)
                    fix_diagonal(i, m)
                    if r == 6:
                        normalise(i, p - 1)
                    if r == 10 and not (final and p == PAIRS - 1):
                        copy_v(i, p + 1)

                dve.sem_inc(score_slots_free, FREE0)
                dve.sem_inc(prob_slots_free, FREE0)
                copy_v(0, 0)
                for m in range(7):
                    fix_diagonal(0, m)
                with dve.Fori(0, ROUNDS) as i:
                    for m in range(7, TPB + 7):
                        tile_step(i, m)
                for m in range(TAIL * TPP + 7, TILES):
                    tile_step(0, m, final=True)
                evacuate(0, PAIRS - 1)
                normalise(0, PAIRS - 1)
                dve.wait_ge(o_kept, PAIRS)
                dve.sem_inc(attn_done, 1)
            with dve.Else():
                dve.wait_ge(g_band_in, 16)
                dve.sem_inc(g_dve, 1)
                chain = Chain(dve, g_dve, G_LINKS)
                with dve.Fori(0, PAIRS) as p:
                    dve.wait_ge(g_loaded, p * 32 + 32)
                    apart(dve)
                    for h in range(2):
                        with dve.Fori(0, NT) as t:
                            n = p * 16 + h * 8 + t
                            chain.start(n, 1)
                            chain.link(nc.vector.tensor_copy(g_q, g_qk[:, 0, h, bass.ds(t * P, P)]))
                            dve.wait_ge(g_pe, n * 3 + 1)
                            chain.link(ts(g_scores, slot[0], SCALE, -CLAMP, ALU.mult, ALU.max))
                            chain.link(ts(g_scores, g_scores, CLAMP, None, ALU.min))
                            chain.link(tt(g_scores, g_scores, g_band[:, bass.ds(t * -P + (S - P), S)], ALU.mult))
                            chain.link(ts(g_scores, g_scores, -CLAMP, CLAMP, ALU.max, ALU.min))
                            chain.link(nc.vector.tensor_reduce(g_stat[:, 0:1], g_scores, AX_X, ALU.max, negate=True))
                            dve.wait_ge(g_act, n + 1)
                            dve.wait_ge(g_pe, n * 3 + 2)
                            chain.link(nc.vector.tensor_copy(g_pT, slot[1]))
                            chain.link(nc.vector.reciprocal(g_stat[:, 2:3], g_stat[:, 1:2]))
                            dve.wait_ge(g_pe, n * 3 + 3)
                            chain.link(ts(xT[:, bass.ds(p * P + (h * 64) + t * HD, HD)], bank[4][:, 0:HD], g_stat[:, 2:3], None, ALU.mult))
                            chain.end()
                dve.sem_inc(attn_done, 1)

            ln = Chain(dve, ln_chain, 2)
            ln2 = Chain(dve, ln2_chain, 2)
            rt = Chain(dve, route_chain, 8)

            def statistics(chain, src, st, m, v, s):
                for t in range(CT):
                    last = nc.vector.bn_stats(st[:, t, :], src[:, t * P:(t + 1) * P])
                chain.link(last)
                apart(dve)
                for t in range(CT):
                    last = nc.vector.bn_aggr(m[:, t, :], st[:, t, :])
                chain.link(last)
                ts(v, m[:, :, 1], EPS, None, ALU.add).then_inc(s, 1)

            def normal_rows(dst, src, m, r):
                for t in range(CT):
                    last = ts(dst[:, t * P:(t + 1) * P], src[:, t * P:(t + 1) * P], m[:, t, 0:1], r[:, t:t + 1], ALU.subtract, ALU.mult)
                return last

            def ln1_statistics(c, i, q):
                ln.start(c)
                dve.wait_ge(c_x[q], i * 16 + 16)
                dve.wait_ge(c_wo, c + 1)
                tt(y_pre[q], bank[7], x_res[q], ALU.add).then_inc(c_y, 1)
                dve.wait_ge(c_y, c + 1)
                statistics(ln, y_pre[q], stats, mv, var, c_var)

            def ln1_rows(c, q):
                dve.wait_ge(c_rstd, c + 1)
                normal_rows(xn[q], y_pre[q], mv, rstd).then_inc(c_xn, 1)

            def route(c, q):
                rt.start(c)
                dve.wait_ge(c_lg, c + 1)
                nc.vector.tensor_copy(logits, bank[7][:, 0:CT * E].rearrange("t (c e) -> t c e", c=CT)).then_inc(c_lgk, 1)
                dve.wait_ge(c_lgk, c + 1)
                apart(dve)
                for t in range(CT):
                    last = nc.vector.max(top8[:, t, :], logits[:, t, :])
                rt.link(last)
                tt(gap, top8[:, :, 1], top8[:, :, 0], ALU.subtract).then_inc(c_gap, 1)
                for t in range(CT):
                    last = nc.vector.max_index(top_i[:, t, :], top8[:, t, :], logits[:, t, :])
                rt.link(last)
                rt.link(nc.vector.tensor_copy(idx_f, top_i))
                lanes = lane8.rearrange("t (c e) -> t c e", c=CT)
                tt(eq1, lanes, idx_f[:, :, 0:1].to_broadcast([P, CT, E]), ALU.is_equal)
                tt(eq2, lanes, idx_f[:, :, 1:2].to_broadcast([P, CT, E]), ALU.is_equal)
                dve.wait_ge(c_exp, c + 1)
                rt.link(ts(w2, gexp, 1.0, None, ALU.add))
                rt.link(nc.vector.reciprocal(w1, w2))
                rt.link(tt(w2, gexp, w1, ALU.mult))
                tt(eq1, eq1, w1.unsqueeze(2).to_broadcast([P, CT, E]), ALU.mult)
                rt.link(tt(eq2, eq2, w2.unsqueeze(2).to_broadcast([P, CT, E]), ALU.mult))
                rt.link(tt(weights[q], eq1, eq2, ALU.add))
                rt.end()

            def hidden(c, e):
                dve.wait_ge(e_silu, c * NE + (e + 1))
                tt(hid[e % 2], silu[e % 2], bank[2 + e % 2], ALU.mult).then_inc(e_hid, 1)

            def weigh(c, q, e):
                dve.wait_ge(e_dn, c * (E + 1) + (e + 1))
                if e >= 2:
                    dve.wait_ge(e_acc, c * E + (e - 1))
                tt(part_e[e % 2].rearrange("t (c d) -> t c d", c=CT), bank[4 + e % 2].rearrange("t (c d) -> t c d", c=CT),
                   weights[q][:, :, e:e + 1].to_broadcast([P, CT, P]), ALU.mult).then_inc(e_part, 1)

            def step(c, i, q, last, previous=True):
                for e in range(NE):
                    hidden(c, e)
                    if e == 1:
                        if previous:
                            finish(c - 1, 1 - q)
                        route(c, q)
                    if 1 <= e <= E:
                        weigh(c, q, e - 1)
                    if not last:
                        if e == 3:
                            ln1_statistics(c + 1, i + q, 1 - q)
                        if e == 4:
                            ln1_rows(c + 1, 1 - q)
                dve.wait_ge(e_dn, c * (E + 1) + (E + 1))
                dve.wait_ge(e_acc, c * E + E)
                dve.wait_ge(c_store[q], i * 16 + 16)
                tt(outb[q], bank[4], acc[q], ALU.add).then_inc(c_shared, 1)

            def finish(c, q):
                ln2.start(c)
                dve.wait_ge(c_shared, c + 2)
                statistics(ln2, outb[q], stats2, mv2, var2, c_var2)
                dve.wait_ge(c_rstd2, c + 1)
                normal_rows(outb[q], outb[q], mv2, rstd2).then_inc(c_out, 1)

            dve.sem_inc(c_shared, 1)
            dve.sem_inc(e_hid, 2)
            ln1_statistics(0, 0, 0)
            ln1_rows(0, 0)
            step(0, 0, 0, False, previous=False)
            with dve.Fori(0, NCH // 2 - 1) as i:
                step(i * 2 + 1, i, 1, False)
                step(i * 2 + 2, i + 1, 0, False)
            step(NCH - 1, NCH // 2 - 1, 1, True)
            finish(NCH - 1, 1)


_INS = ["L0_attn_x", "L0_attn_Wq", "L0_attn_Wk", "L0_attn_Wv", "L0_attn_Wo", "L0_attn_W_down_kv", "L0_attn_W_up_k",
        "L0_attn_W_up_v", "L0_ffn_w_router", "L0_ffn_fc1_w", "L0_ffn_fc2_w", "L0_ffn_gate_w", "L0_ffn_up_w", "L0_ffn_down_w"]


def kernel(**inputs):
    import concourse.bacc as _bacc
    from concourse.bass_utils import run_bass_kernel_spmd as _run

    nc = _bacc.Bacc("TRN2", target_bir_lowering=False, num_devices=1)
    shape = inputs["L0_attn_x"].shape
    consts = dict(zip(("decay_rows", "const_pack", "decay_band"), shape_constants(shape[1], shape[2])))
    arrays, args = {}, []
    for name, a in [(n, inputs[n]) for n in _INS] + list(consts.items()):
        a = np.ascontiguousarray(a)
        arrays[f"in_{name}"] = a
        args.append(nc.dram_tensor(f"in_{name}", a.shape, mybir.dt.from_np(a.dtype), kind="ExternalInput").ap())
    out = nc.dram_tensor("out_0", shape, F32, kind="ExternalOutput").ap()
    block_kernel(nc, *args, out)
    r = _run(nc, [arrays], core_ids=[0])
    return r.results[0]["out_0"]
```

```python
from contextlib import ExitStack

import numpy as np

import concourse.bass as bass
from concourse import mybir

F32 = mybir.dt.float32
BF16 = mybir.dt.bfloat16
I32 = mybir.dt.int32
U32 = mybir.dt.uint32
ALU = mybir.AluOpType
ACT = mybir.ActivationFunctionType
AX_X = mybir.AxisListType.X

P = 128
HEADS = 16
HD = 8
CLAMP = 10000.0
DECAY_RATE = 0.01 * 0.01
EPS = 1e-5
SCORE_LIMIT = 40.0
SUM_LIMIT = 1e16
NPART = 3


def shape_constants(S, D):
    pos = np.arange(S, dtype=np.float64) - S // 2
    rows = np.stack([np.exp(-DECAY_RATE * pos), np.exp(DECAY_RATE * pos)]).astype(np.float32)
    j, i = np.arange(P)[:, None].astype(np.float64), np.arange(P)[None, :].astype(np.float64)
    diag = np.exp(-2 * DECAY_RATE * np.maximum(j - i, 0.0))
    head_sum = np.zeros((P, 32))
    head_sum[np.arange(D), 2 * (np.arange(D) // (2 * HD)) + np.arange(D) % 2] = 1.0
    lane = np.tile(np.arange(8, dtype=np.float64), (P, 4))
    pack = np.concatenate([np.eye(P), diag, head_sum, lane, np.ones((P, 1))], axis=1).astype(np.float32)
    c = np.arange(2 * S - P, dtype=np.float64)[None, :]
    band = np.exp(-DECAY_RATE * np.abs(c - j - (S - P))).astype(np.float32)
    return rows, pack, band


def block_kernel(nc, x, Wq, Wk, Wv, Wo, Wd, Wuk, Wuv, Wr, fc1, fc2, gate_w, up_w, down_w,
                 decay_rows, const_pack, decay_band, out):
    B, S, D = x.shape
    L = Wd.shape[1]
    E, _, F2 = fc1.shape
    F = F2 // 2
    NT = S // P
    HALF = S // 2
    CT = HALF // P
    PAIRS = B * HEADS // 2
    PPB = HEADS // 2
    NCH = B * 2
    NE = E + gate_w.shape[1] // F
    SCALE = float(np.float32(1.0) / (np.sqrt(np.float32(D)) + np.float32(1e-8)))
    NORM_LIMIT = (SCORE_LIMIT / SCALE) ** 2
    assert D == P and HEADS * HD == P and F == P and S == 1024 and PPB == NT and NE == E + 2

    x_tiles = x.rearrange("b (t p) d -> b p t d", p=P)
    x_rows = x.rearrange("b s d -> (b s) d")
    out_rows = out.rearrange("b s d -> (b s) d")

    parts_dram = nc.dram_tensor("parts_dram", (2, NPART, B * P, 2 * S), BF16, kind="Internal").ap()
    raw_dram = nc.dram_tensor("raw_dram", (2, B * P, S), F32, kind="Internal").ap()

    with ExitStack() as ctx:
        def sb(name, shape, dt=F32):
            return ctx.enter_context(nc.sbuf_tensor(name, shape, dt))

        def sem(name):
            return ctx.enter_context(nc.semaphore(name))

        xT = sb("xT", [P, B * S])
        attn_pair = xT[:, :].rearrange("t (p g c d) -> t p g c d", p=PAIRS, g=4, c=CT)
        attn_chunk = xT[:, :].rearrange("t (b x h c d) -> t b h c x d", b=B, x=HEADS, h=2, c=CT)
        qT = sb("qT", [P, B * S])
        kT = sb("kT", [P, B * S])
        qkT = (qT, kT)
        V_all = sb("V_all", [P, PAIRS, NT, 2 * HD])
        stacks = sb("stacks", [P, 3 * 2 * 2 * 2 * S], BF16)
        sv = stacks[:, :].rearrange("r (u k h v s) -> r u k h v s", u=3, k=2, h=2, v=2)
        probs = sb("probs", [P, 6, S])
        stage = sb("stage", [P, 2, NPART, 2 * S], BF16)
        ptmp = sb("ptmp", [P, 2, S])
        rows_sb = sb("rows_sb", [P, 2, S])
        cpk = sb("cpk", [P, const_pack.shape[1]])
        Vring = sb("Vring", [P, 3, NT, 2, 32])
        osb = sb("osb", [P, HALF])
        rec = sb("rec", [P, 16])
        Wq_sb = sb("Wq_sb", [P, D])
        Wq_turned = sb("Wq_turned", [P, D])
        Wkv_sb = sb("Wkv_sb", [P, 3, D])
        Wd_sb = sb("Wd_sb", [P, L])
        Wu_sb = sb("Wu_sb", [L, 2, D])
        wfold = sb("wfold", [P, 4, D])
        sq = sb("sq", [P, 2, 2, HALF], BF16)
        head_sum_h = sb("head_sum_h", [P, 32], BF16)
        sqv = osb[:, :]
        sums = sb("sums", [P, 3 * NCH])
        nmax = sb("nmax", [64, NCH])
        test = sb("test", [P, 8])
        testv = sb("testv", [P, 3 * NCH])
        flag = sb("flag", [1, 1], I32)
        Wo_sb = sb("Wo_sb", [P, D])
        Wr_sb = sb("Wr_sb", [P, E])
        late = stage[:, :, :, :].rearrange("p k a s -> p (k a s)").bitcast(F32)
        up_sb = late[:, 0:NE * 2 * F].rearrange("p (e n) -> p e n", e=NE)
        dn_sb = late[:, NE * 2 * F:NE * (2 * F + D)].rearrange("p (e n) -> p e n", e=NE)
        small = sb("small", [P, 512])

        ident = cpk[:, 0:P]
        diag_fix = cpk[:, P:2 * P]
        head_sum = cpk[:, 2 * P:2 * P + 32]
        lane8 = cpk[:, 2 * P + 32:2 * P + 64]
        ones = cpk[:, 2 * P + 64:2 * P + 65]

        x_tok = probs[:, 0:B, :]
        gflat = stacks[:, :].bitcast(F32)
        g_qk = gflat[0:HD, 0:4 * S].rearrange("d (k h s) -> d k h s", k=2, h=2)
        g_band = gflat[:, 4 * S:4 * S + 2 * S - P]
        g_q = gflat[0:HD, 6 * S:6 * S + P]
        g_scores, g_probs, g_pT = probs[:, 0, :], probs[:, 1, :], probs[:, 2, :]
        g_stat = test[:, 4:8]
        NB = HALF
        ev = [gflat[:, n * NB:(n + 1) * NB] for n in range(22)]
        x_res = [ptmp[:, 0, q * NB:(q + 1) * NB] for q in range(2)]
        a_chunk = [ptmp[:, 1, q * NB:(q + 1) * NB] for q in range(2)]
        y_pre, xn, xnT, aT = ((ev[16 + n], ev[n]) for n in range(4))
        outb, silu, part_e, acc = (ev[4 + 2 * n:6 + 2 * n] for n in range(4))
        hid = ev[12:15]

        ps = ctx.enter_context(nc.psum_tensor("ps", [P, 8, HALF], F32))
        bank = [ps[:, n, :] for n in range(8)]
        slot = [ps[:, 2 * n:2 * n + 2, :].rearrange("p a b -> p (a b)") for n in range(3)]

        s_pack, s_rows, s_wkv, s_wq, s_late_first, s_late = (sem(n) for n in ("pack_loaded", "rows_loaded", "wkv_loaded", "wq_loaded", "wo_wr_loaded", "expert_weights_loaded"))
        s_x = [sem(f"x_loaded{b}") for b in range(B)]
        wq_turned = sem("wq_turned")
        wkv_added, fold_done, fold_copied = sem("wkv_added"), sem("fold_done"), sem("fold_copied")
        xT_ready, xT_copied = sem("xT_ready"), sem("xT_copied")
        qk_ready, qk_kept = sem("qk_ready"), sem("qk_kept")
        v_ready, v_kept, v_squared = sem("v_ready"), sem("v_kept"), sem("v_squared")
        norm_ready, norm_maxed = sem("norm_ready"), sem("norm_maxed")
        prep_chain, stage_stored = sem("prep_chain"), sem("stage_stored")
        stage_ready = [sem("stage_ready_q"), sem("stage_ready_k")]
        stage_k_rest = sem("stage_ready_k_rest")
        test_ready, test_summed, flag_ready = sem("test_ready"), sem("test_summed"), sem("flag_ready")
        pad_zeroed, pads_zeroed = sem("pad_zeroed_by_dve"), sem("pads_zeroed_by_pool")
        pool_chain = sem("pool_chain")
        pool_stored = [sem("pool_stored_q"), sem("pool_stored_k")]
        pairs_stored = sem("pairs_stored")
        stack_loaded = [sem(f"stack_loaded{u}") for u in range(3)]

        scores_ready, diag_done = sem("scores_ready"), sem("diag_done")
        score_slots_free, prob_slots_free = sem("score_slots_free"), sem("prob_slots_free")
        v_copied, o_evacuated, o_turned, rec_done, o_kept = (sem(n) for n in ("v_copied", "o_evacuated", "o_turned", "rec_done", "o_kept"))
        g_raw, g_loaded, g_band_in, g_dve, g_pe, g_act = (sem(n) for n in ("g_raw", "g_loaded", "g_band_in", "g_dve", "g_pe", "g_act"))
        apart_ticks = sem("apart_ticks")
        attn_done = sem("attn_done")
        c_x = [sem("chunk_x0"), sem("chunk_x1")]
        c_a, c_aT, c_aTk, c_wo, c_y = (sem(n) for n in ("a_gathered", "a_turned", "a_kept", "wo_ready", "y_done"))
        c_lgk, pool_const, ln_chain, ln2_chain, route_chain = (sem(n) for n in ("logits_kept", "pool_const", "ln_chain", "ln2_chain", "route_chain"))
        c_var, c_rstd, c_xn, c_xnT, c_xnTk, c_lg = (sem(n) for n in ("var_done", "rstd_done", "xn_done", "xn_turned", "xn_kept", "logits_ready"))
        c_gap, c_exp = sem("gap_done"), sem("gap_exp")
        e_up, e_silu, e_hid, e_dn, e_part, e_acc = (sem(n) for n in ("up_ready", "silu_done", "hidden_done", "down_ready", "part_done", "acc_done"))
        c_shared, c_var2, c_rstd2, c_out = sem("shared_done"), sem("var2_done"), sem("rstd2_done"), sem("out_done")
        c_store = [sem("stored0"), sem("stored1")]

        block = ctx.enter_context(nc.Block())

        BODY_PAIRS = 3
        TPP = 2 * NT
        TPB = BODY_PAIRS * TPP
        ROUNDS = (PAIRS - 2) // BODY_PAIRS
        TAIL = ROUNDS * BODY_PAIRS
        K_SHARE = 3 * S // 4
        FREE0 = 3
        LOADS = 2 * NPART * 16
        TILES = PAIRS * TPP
        G_LINKS = 9

        def apart(eng):
            eng.sem_inc(apart_ticks, 1)

        class Chain:

            def __init__(self, eng, s, per_call):
                self.eng, self.s, self.per_call = eng, s, per_call

            def start(self, call, offset=0):
                self.base, self.k = call * self.per_call + offset, 0

            def link(self, ins, wait=True):
                self.k += 1
                ins.then_inc(self.s, 1)
                if wait:
                    self.eng.wait_ge(self.s, self.base + self.k)

            def end(self):
                assert self.k == self.per_call, self.k

        at = [0]

        def small_tile(n, *dims):
            at[0] += n
            v = small[:, at[0] - n:at[0]]
            return v.rearrange("p (c k) -> p c k", c=CT) if dims else v

        stats = small_tile(CT * 6, 1)
        mv = small_tile(CT * 2, 1)
        stats2 = small_tile(CT * 6, 1)
        mv2 = small_tile(CT * 2, 1)
        var, rstd, var2, rstd2, gap, gexp, mhalf, ebase, w1, w2 = (small_tile(CT) for _ in range(10))
        logits, top8, idx_f, eq1, eq2 = (small_tile(CT * 8, 1) for _ in range(5))
        top_i = small_tile(CT * 8, 1).bitcast(U32)
        weights = [small_tile(CT * 8, 1) for _ in range(2)]

        @block.sync
        def _(sp):
            def load_x(b):
                sp.dma_start(x_tok[:, b, :].rearrange("p (t d) -> p t d", t=NT), x_tiles[b]).then_inc(s_x[b], 16)

            sp.dma_start(cpk[:, :], const_pack).then_inc(s_pack, 16)
            load_x(0)
            sp.dma_start(Wkv_sb[:, 0, :], Wk).then_inc(s_wkv, 16)
            sp.dma_start(Wkv_sb[:, 1, :], Wv).then_inc(s_wkv, 16)
            sp.dma_start(Wd_sb[:, :], Wd).then_inc(s_wkv, 16)
            sp.dma_start(Wu_sb[:, 0, :], Wuk).then_inc(s_wkv, 16)
            sp.dma_start(Wu_sb[:, 1, :], Wuv).then_inc(s_wkv, 16)
            sp.dma_start(Wq_sb[:, :], Wq).then_inc(s_wq, 16)
            for b in range(1, B):
                load_x(b)
            for v in range(2):
                sp.dma_start(rows_sb[:, v, :], decay_rows[v:v + 1, :].to_broadcast([P, S])).then_inc(s_rows, 16)
            sp.dma_start(Wo_sb[:, :], Wo).then_inc(s_late_first, 16)
            sp.dma_start(Wr_sb[:, :], Wr).then_inc(s_late_first, 16)
            for v in range(2):
                for n in range(2):
                    sp.wait_ge(stage_ready[n], v + 1)
                    if n and v:
                        sp.wait_ge(stage_k_rest, 1)
                    sp.dma_start(parts_dram[n, :, 0:P, v * S:(v + 1) * S].rearrange("a r s -> r a s"),
                                 stage[:, n, :, v * S:(v + 1) * S]).then_inc(stage_stored, 16)

            def load_pair(p, u):
                here = bass.ds(p * 2 * HD, 2 * HD)
                for a in range(NPART):
                    rows = slice(a * NPART * HD, (a + 1) * NPART * HD)
                    q_part = parts_dram[0, a:a + 1, here, :].rearrange("a (d h) s -> a d (h s)", h=2)
                    k_parts = parts_dram[1, :, here, :].rearrange("b (d h) s -> b d (h s)", h=2)
                    for n, src in ((0, q_part.to_broadcast([NPART, HD, 4 * S])), (1, k_parts)):
                        dst = sv[rows, u, n, :, :, :].rearrange("r h v s -> r (h v s)")
                        sp.dma_start(dst, src).then_inc(stack_loaded[u], 16)

            sp.wait_ge(stage_stored, 64)
            sp.wait_ge(pad_zeroed, 1)
            sp.wait_ge(pads_zeroed, 2)
            for p in range(BODY_PAIRS):
                load_pair(p, p)

            sp.wait_ge(flag_ready, 1)
            fits = sp.value_load(flag[0:1, 0:1], min_val=0, max_val=P)
            with sp.If(fits >= P):
                with sp.Fori(1, ROUNDS) as i:
                    for u in range(BODY_PAIRS):
                        sp.wait_ge(scores_ready, i * TPB + (u - 2) * TPP)
                        apart(sp)
                        sp.wait_ge(pairs_stored, i * 3 + (u + 1))
                        load_pair(i * 3 + u, u)
                for p in range(TAIL, PAIRS):
                    sp.wait_ge(scores_ready, (p - 2) * TPP)
                    sp.wait_ge(pairs_stored, p + 1)
                    load_pair(p, p % 3)
                sp.wait_ge(pairs_stored, PAIRS)
            with sp.Else():
                for u in range(BODY_PAIRS):
                    sp.wait_ge(stack_loaded[u], LOADS)
                sp.wait_ge(qk_kept, 4 * B)
                sp.dma_start(g_band, decay_band).then_inc(g_band_in, 16)
                for n in range(2):
                    sp.dma_start(raw_dram[n].rearrange("(b r) s -> r b s", b=B),
                                 qkT[n][:, :].rearrange("r (b s) -> r b s", b=B)).then_inc(g_raw, 16)
                sp.wait_ge(g_raw, 32)
                with sp.Fori(0, PAIRS) as p:
                    sp.wait_ge(g_dve, p * (16 * G_LINKS) + 1)
                    for n in range(2):
                        sp.dma_start(g_qk[:, n, :, :],
                                     raw_dram[n, bass.ds(p * 2 * HD, 2 * HD), :].rearrange("(d h) s -> d h s", h=2)).then_inc(g_loaded, 16)

            sp.wait_ge(stage_stored, 64)
            sp.dma_start(up_sb[:, 0:E, :], fc1.rearrange("e h n -> h e n")).then_inc(s_late, 16)
            sp.dma_start(dn_sb[:, 0:E, :], fc2.rearrange("e i h -> i e h")).then_inc(s_late, 16)
            sp.dma_start(up_sb[:, E:NE, 0:F], gate_w.rearrange("h (j n) -> h j n", j=2)).then_inc(s_late, 16)
            sp.dma_start(up_sb[:, E:NE, F:2 * F], up_w.rearrange("h (j n) -> h j n", j=2)).then_inc(s_late, 16)
            sp.dma_start(dn_sb[:, E:NE, :], down_w.rearrange("(j i) h -> i j h", j=2)).then_inc(s_late, 16)

            def chunk_io(c, q, first):
                if not first:
                    sp.wait_ge(c_y, c - 1)
                sp.dma_start(x_res[q].rearrange("p (t d) -> p t d", t=CT),
                             x_rows[bass.ds(c * HALF, HALF), :].rearrange("(t p) d -> p t d", p=P)).then_inc(c_x[q], 16)

            def chunk_store(c, q):
                sp.wait_ge(c_out, c + 1)
                sp.dma_start(out_rows[bass.ds(c * HALF, HALF), :].rearrange("(t p) d -> p t d", p=P),
                             outb[q].rearrange("p (t d) -> p t d", t=CT)).then_inc(c_store[q], 16)

            for q in range(2):
                sp.sem_inc(c_store[q], 16)
            chunk_io(0, 0, True)
            chunk_io(1, 1, True)
            with sp.Fori(0, NCH // 2 - 1) as i:
                for q in range(2):
                    chunk_io(i * 2 + (q + 2), q, False)
                    chunk_store(i * 2 + q, q)
            for q in range(2):
                chunk_store(NCH - 2 + q, q)
            for q in range(2):
                sp.wait_ge(c_store[q], 16 * NCH // 2 + 16)


        @block.gpsimd
        def _(pool):
            def split(src, n, v, k0, tokens=S):
                tab = rows_sb[:, v ^ n, 0:tokens]
                hi, mid, lo = (stage[:, n, a, v * S:v * S + tokens] for a in range(NPART))
                f, r = ptmp[:, 0, 0:tokens], ptmp[:, 1, 0:tokens]
                nc.gpsimd.tensor_tensor(f, src, tab, ALU.mult).then_inc(pool_chain, 1)
                nc.gpsimd.tensor_tensor(hi, src, tab, ALU.mult).then_inc(pool_chain, 1)
                pool.wait_ge(pool_chain, k0 + 2)
                nc.gpsimd.tensor_tensor(r, f, hi, ALU.subtract).then_inc(pool_chain, 1)
                nc.gpsimd.tensor_tensor(mid, f, hi, ALU.subtract).then_inc(pool_chain, 1)
                pool.wait_ge(pool_chain, k0 + 4)
                nc.gpsimd.tensor_tensor(lo, r, mid, ALU.subtract).then_inc(pool_chain, 1)
                pool.wait_ge(pool_chain, k0 + 5)

            for u in range(1, 3):
                nc.gpsimd.memset(sv[64:P, u].rearrange("r k h v s -> r (k h v s)").bitcast(F32), 0.0).then_inc(pads_zeroed, 1)
                pool.wait_ge(pads_zeroed, u)
            pool.wait_ge(s_wq, 16)
            for h in range(2):
                nc.gpsimd.tensor_copy(Wq_turned[:, :].rearrange("p (g d h) -> p h g d", g=PPB, h=2)[:, h],
                                      Wq_sb[:, :].rearrange("p (g h d) -> p h g d", g=PPB, h=2)[:, h]).then_inc(wq_turned, 1)
            pool.wait_ge(s_rows, 32)
            pool.wait_ge(qk_kept, 4)
            for v, tokens in ((0, S), (1, K_SHARE)):
                split(kT[:, 0:tokens], 1, v, v * 5, tokens)
                pool.sem_inc(stage_ready[1], 1)

            pool.wait_ge(flag_ready, 1)
            fits = pool.value_load(flag[0:1, 0:1], min_val=0, max_val=P)
            with pool.If(fits >= P):
                pool.wait_ge(stage_stored, 64)
                pool.sem_inc(pairs_stored, PPB)
                with pool.Fori(1, B) as b:
                    for n in range(2):
                        for v in range(2):
                            split(qkT[n][:, bass.ds(b * S, S)], n, v, b * 20 + (n * 10 + v * 5 - 10))
                            apart(pool)
                        pool.dma_start(parts_dram[n, :, bass.ds(b * P, P), :].rearrange("a r s -> r a s"),
                                       stage[:, n, :, :]).then_inc(pool_stored[n], 16)
                    for n in range(2):
                        pool.wait_ge(pool_stored[n], b * 16)
                    pool.sem_inc(pairs_stored, PPB)
                pool.wait_ge(o_kept, PPB)
            with pool.Else():
                pool.wait_ge(attn_done, 1)

            nc.gpsimd.memset(mhalf, -0.5).then_inc(pool_const, 1)
            nc.gpsimd.memset(ebase, float(np.e)).then_inc(pool_const, 1)
            pool.wait_ge(pool_const, 2)

            def gather(c, b, q, first=False):
                if not first:
                    pool.wait_ge(c_xnTk, c - 1)
                nc.gpsimd.tensor_copy(a_chunk[q].rearrange("t (o c h d) -> t o c h d", o=1, c=CT, h=HEADS),
                                      attn_chunk[:, bass.ds(b, 1), q, :, :, :]).then_inc(c_a, 1)

            def ln_power(c):
                pool.wait_ge(c_var, c + 1)
                nc.gpsimd.tensor_tensor(rstd, var, mhalf, ALU.pow).then_inc(c_rstd, 1)

            def gap_power(c):
                pool.wait_ge(c_gap, c + 1)
                nc.gpsimd.tensor_tensor(gexp, ebase, gap, ALU.pow).then_inc(c_exp, 1)

            def step(c, b, q, last, previous=True):
                if previous and not last:
                    gather(c + 1, b + q, 1 - q)
                if previous:
                    finish(c - 1)
                for e in range(E):
                    if e == E - 1 and not last:
                        gap_power(c + 1)
                    pool.wait_ge(e_part, c * E + (e + 1))
                    if e:
                        pool.wait_ge(e_acc, c * E + e)
                    nc.gpsimd.tensor_tensor(acc[q], xn[q] if e == 0 else acc[q], part_e[e % 2], ALU.add).then_inc(e_acc, 1)
                    if e == 3 and not last:
                        ln_power(c + 1)

            def finish(c):
                pool.wait_ge(c_var2, c + 1)
                nc.gpsimd.tensor_tensor(rstd2, var2, mhalf, ALU.pow).then_inc(c_rstd2, 1)

            for q in range(2):
                gather(q, 0, q, first=True)
            ln_power(0)
            gap_power(0)
            step(0, 0, 0, False, previous=False)
            with pool.Fori(0, NCH // 2 - 1) as i:
                step(i * 2 + 1, i, 1, False)
                step(i * 2 + 2, i + 1, 0, False)
            step(NCH - 1, NCH // 2 - 1, 1, True)
            finish(NCH - 1)

        @block.scalar
        def _(act):
            def keep_xT(b):
                for h in range(2):
                    act.wait_ge(xT_ready, 2 * b + h + 1)
                    nc.scalar.activation(xT[:, b * S + h * HALF:b * S + (h + 1) * HALF], bank[h], ACT.Copy).then_inc(xT_copied, 1)

            keep_xT(0)
            def turned(ap, order):
                return [ap.rearrange(f"p ({order}) -> p h g d", g=PPB, h=2)[:, h] for h in range(2)]

            k_weight = list(zip(turned(wfold[:, 2, :], "g d h"), turned(bank[4][:, 0:P], "g h d")))
            for done, copies in ((1, [(wfold[:, 0, :], bank[2][:, 0:P])]), (2, [(wfold[0:L, 1, :], bank[3][0:L, 0:P])]),
                                 (3, k_weight), (4, [(wfold[:, 3, :], bank[5][:, 0:P])])):
                act.wait_ge(fold_done, done)
                for dst, src in copies:
                    nc.scalar.activation(dst, src, ACT.Copy).then_inc(fold_copied, 1)
            for b in range(B):
                for h in range(2):
                    if b:
                        act.wait_ge(norm_ready, 2 * b + h - 1)
                    for n in range(2):
                        act.wait_ge(qk_ready, 4 * b + 2 * h + n + 1)
                        src = bank[2 + 2 * h + n]
                        nc.scalar.activation(qkT[n][:, b * S + h * HALF:b * S + (h + 1) * HALF], src, ACT.Copy)
                        k = n * NCH + 2 * b + h
                        nc.scalar.activation(sq[:, h, n, :], src, ACT.Square, accum_out=sums[:, k:k + 1]).then_inc(qk_kept, 1)
                if b < B - 1:
                    keep_xT(b + 1)
                for h in range(2):
                    act.wait_ge(v_kept, 2 * b + h + 1)
                    if b or h:
                        act.wait_ge(v_squared, 2 * b + h)
                    k = 2 * NCH + 2 * b + h
                    nc.scalar.activation(sqv.rearrange("p (w t e) -> p w t e", w=PPB, t=CT),
                                         V_all[:, b * PPB:(b + 1) * PPB, CT * h:CT * (h + 1), :], ACT.Square,
                                         accum_out=sums[:, k:k + 1]).then_inc(v_squared, 1)

            def keep_a(c, q, src=bank[6]):
                act.wait_ge(c_aT, c + 1)
                nc.scalar.activation(aT[q], src, ACT.Copy).then_inc(c_aTk, 1)

            def keep_x(c, q, src=bank[6]):
                act.wait_ge(c_xnT, c + 1)
                nc.scalar.activation(xnT[q], src, ACT.Copy).then_inc(c_xnTk, 1)

            act.wait_ge(flag_ready, 1)
            fits = act.value_load(flag[0:1, 0:1], min_val=0, max_val=P)
            with act.If(fits >= P):
                with act.Fori(0, ROUNDS) as i:
                    for m in range(TPB):
                        if m % 2 == 0:
                            act.wait_ge(prob_slots_free, i * (TPB // 2) + (m // 2 + 1))
                        act.wait_ge(diag_done, i * TPB + (m + 1))
                        nc.scalar.activation(probs[:, m % 6, :], slot[m % 3], ACT.Exp, scale=SCALE).then_inc(score_slots_free, 1)
                for m in range(TAIL * TPP, TILES):
                    if m % 2 == 0:
                        act.wait_ge(prob_slots_free, m // 2 + 1)
                    act.wait_ge(diag_done, m + 1)
                    nc.scalar.activation(probs[:, m % 6, :], slot[m % 3], ACT.Exp, scale=SCALE).then_inc(score_slots_free, 1)
                    if m == TILES - TPP - 3:
                        keep_a(0, 0, bank[7])
                    if m == TILES - 3:
                        keep_x(0, 0, bank[7])
            with act.Else():
                with act.Fori(0, PAIRS * 2 * NT) as n:
                    act.wait_ge(g_dve, n * G_LINKS + 7)
                    nc.scalar.activation(g_probs, g_scores, ACT.Exp, bias=g_stat[:, 0:1],
                                         accum_out=g_stat[:, 1:2]).then_inc(g_act, 1)
                keep_a(0, 0, bank[7])
                keep_x(0, 0, bank[7])

            def step(c, b, q, last):
                for e in range(NE):
                    act.wait_ge(e_up, c * NE + (e + 1))
                    nc.scalar.activation(silu[e % 2], bank[e % 2], ACT.Silu).then_inc(e_silu, 1)
                    if e == 2 and not last:
                        keep_a(c + 1, 1 - q)
                    if e == 8 and not last:
                        keep_x(c + 1, 1 - q)

            step(0, 0, 0, False)
            with act.Fori(0, NCH // 2 - 1) as i:
                step(i * 2 + 1, i, 1, False)
                step(i * 2 + 2, i + 1, 0, False)
            step(NCH - 1, NCH // 2 - 1, 1, True)

        @block.tensor
        def _(pe):
            mm = nc.tensor.matmul
            def turn_batch(b):
                pe.wait_ge(s_x[b], 16)
                for h in range(2):
                    for t in range(CT):
                        last = nc.tensor.transpose(bank[h][:, t * P:(t + 1) * P],
                                                   x_tok[:, b, (h * CT + t) * P:(h * CT + t + 1) * P], ident)
                    last.then_inc(xT_ready, 1)

            pe.wait_ge(s_pack, 16)
            turn_batch(0)
            pe.wait_ge(wkv_added, 1)
            nc.tensor.transpose(bank[2][:, 0:P], Wkv_sb[:, 2, :], ident).then_inc(fold_done, 1)
            pe.wait_ge(fold_copied, 1)
            mm(bank[3][0:L, 0:P], Wd_sb[:, :], wfold[:, 0, :], start=True, stop=True).then_inc(fold_done, 1)
            pe.wait_ge(fold_copied, 2)
            for n in range(2):
                mm(bank[4 + n][:, 0:P], wfold[0:L, 1, :], Wu_sb[:, n, :], start=True, stop=True).then_inc(fold_done, 1)
            pe.wait_ge(fold_copied, 5)
            pe.wait_ge(wq_turned, 2)
            for b in range(B):
                for h in range(2):
                    pe.wait_ge(xT_copied, 2 * b + h + 1)
                    if b:
                        pe.wait_ge(qk_kept, 4 * (b - 1) + 2 * h + 2)
                    rhs = xT[:, b * S + h * HALF:b * S + (h + 1) * HALF]
                    mm(bank[2 + 2 * h], Wq_turned[:, :], rhs, start=True, stop=True).then_inc(qk_ready, 1)
                    mm(bank[3 + 2 * h], wfold[:, 2, :], rhs, start=True, stop=True).then_inc(qk_ready, 1)
                if b < B - 1:
                    turn_batch(b + 1)
                for h in range(2):
                    if b or h:
                        pe.wait_ge(v_kept, 2 * b + h)
                    for t in range(CT):
                        k = b * S + (h * CT + t) * P
                        last = mm(bank[7][:, t * P:(t + 1) * P], xT[:, k:k + P], wfold[:, 3, :], start=True, stop=True)
                    last.then_inc(v_ready, 1)
                    pe.wait_ge(qk_kept, 4 * b + 2 * h + 2)
                    pe.wait_ge(norm_maxed, 2 * b + h + 1)
                    for n in range(2):
                        last = mm(bank[6][32 * n:32 * n + 32, :], head_sum_h[:, :], sq[:, h, n, :], start=True, stop=True)
                    last.then_inc(norm_ready, 1)
            pe.wait_ge(test_ready, 1)
            mm(bank[0][0:1, 0:1], test[:, 2:3], ones, start=True, stop=True).then_inc(test_summed, 1)

            def turn_a(c, q, dst=bank[6]):
                pe.wait_ge(c_a, c + 1)
                for t in range(CT):
                    last = nc.tensor.transpose(dst[:, t * P:(t + 1) * P], a_chunk[q][:, t * P:(t + 1) * P], ident)
                last.then_inc(c_aT, 1)

            def project(c, q):
                pe.wait_ge(c_aTk, c + 1)
                for t in range(CT):
                    last = mm(bank[7][:, t * P:(t + 1) * P], aT[q][:, t * P:(t + 1) * P], Wo_sb[:, :], start=True, stop=True)
                last.then_inc(c_wo, 1)

            def turn_x(c, q, dst=bank[6]):
                pe.wait_ge(c_xn, c + 1)
                for t in range(CT):
                    last = nc.tensor.transpose(dst[:, t * P:(t + 1) * P], xn[q][:, t * P:(t + 1) * P], ident)
                last.then_inc(c_xnT, 1)

            def up(c, q, e):
                pe.wait_ge(e_hid, c * NE + (e + 1))
                if e == 0:
                    pe.wait_ge(c_xnTk, c + 1)
                mm(bank[e % 2], up_sb[:, e, 0:F], xnT[q], start=True, stop=True)
                mm(bank[2 + e % 2], up_sb[:, e, F:2 * F], xnT[q], start=True, stop=True).then_inc(e_up, 1)

            pe.wait_ge(flag_ready, 1)
            fits = pe.value_load(flag[0:1, 0:1], min_val=0, max_val=P)
            with pe.If(fits >= P):
                def score_tile(i, m):
                    u, kt, h = (m // TPP) % BODY_PAIRS, (m % TPP) // 2, m % 2
                    if m % TPP == 0:
                        pe.wait_ge(stack_loaded[u], (i + m // TPB) * LOADS + LOADS)
                    pe.wait_ge(score_slots_free, i * TPB + (m + 1))
                    cuts = sorted({0, kt * P, HALF, S})
                    for lo, hi in zip(cuts, cuts[1:]):
                        v = 0 if lo >= kt * P else 1
                        last = mm(slot[m % 3][:, lo:hi], sv[:, u, 1, h, v, kt * P:(kt + 1) * P], sv[:, u, 0, h, v, lo:hi],
                                  start=True, stop=True)
                    last.then_inc(scores_ready, 1)

                def output_group(i, g):
                    u, kt = (g // NT) % BODY_PAIRS, g % NT
                    if kt == 0:
                        pe.wait_ge(v_copied, i * BODY_PAIRS + (g // NT + 1))
                        if g:
                            pe.wait_ge(o_evacuated, i * BODY_PAIRS + g // NT)
                    pe.wait_ge(score_slots_free, i * TPB + (2 * g + 2 + FREE0))
                    for h in range(2):
                        for qh in range(2):
                            r = 32 * (2 * h + qh)
                            last = mm(bank[6][r:r + 32, :], Vring[:, u, kt, h, :],
                                      probs[:, (2 * g + h) % 6, qh * HALF:(qh + 1) * HALF], start=(kt == 0), stop=(kt == NT - 1))
                    last.then_inc(prob_slots_free, 1)

                def turn_output(i, p):
                    pe.wait_ge(o_evacuated, i * BODY_PAIRS + (p + 1))
                    for c in range(CT):
                        last = nc.tensor.transpose(bank[7][:, c * P:(c + 1) * P], osb[:, c * P:(c + 1) * P], ident)
                    last.then_inc(o_turned, 1)

                LAST = (PAIRS - 1) * NT

                def chunk_0(g):
                    if g == LAST - 3:
                        pe.wait_ge(s_late_first, 2 * 16)
                        pe.wait_ge(o_kept, PAIRS - 2)
                        turn_a(0, 0, bank[7])
                    if g == LAST - 1:
                        project(0, 0)
                    if g == LAST:
                        pe.wait_ge(c_y, 1)
                    if g == LAST + 5:
                        pe.wait_ge(o_kept, PAIRS - 1)
                        turn_x(0, 0, bank[7])

                def group_step(i, g, tiles_left=True):
                    if tiles_left or 2 * g + 4 < TILES:
                        score_tile(i, 2 * g + 4)
                    if not tiles_left:
                        chunk_0(g)
                    if g % NT == 0 and g:
                        turn_output(i, g // NT - 1)
                    output_group(i, g)
                    if tiles_left or 2 * g + 5 < TILES:
                        score_tile(i, 2 * g + 5)

                for m in range(4):
                    score_tile(0, m)
                group_step(0, 0)
                with pe.Fori(0, ROUNDS) as i:
                    for g in range(1, TPB // 2 + 1):
                        group_step(i, g)
                for g in range(TAIL * NT + 1, TILES // 2):
                    group_step(0, g, tiles_left=False)
                pe.wait_ge(s_late, 5 * 16)
                up(0, 0, 0)
                turn_output(0, PAIRS - 1)
                up(0, 0, 1)
            with pe.Else():
                with pe.Fori(0, PAIRS) as p:
                    for h in range(2):
                        with pe.Fori(0, NT) as t:
                            n = p * 16 + h * 8 + t
                            pe.wait_ge(g_dve, n * G_LINKS + 2)
                            for k in range(2):
                                last = mm(bank[k], g_q, g_qk[:, 1, h, k * HALF:(k + 1) * HALF], start=True, stop=True)
                            last.then_inc(g_pe, 1)
                            pe.wait_ge(g_act, n + 1)
                            for k in range(NT):
                                last = nc.tensor.transpose(slot[1][:, k * P:(k + 1) * P], g_probs[:, k * P:(k + 1) * P], ident)
                            last.then_inc(g_pe, 1)
                            pe.wait_ge(g_dve, n * G_LINKS + 8)
                            for k in range(NT):
                                last = mm(bank[4][:, 0:HD], g_pT[:, k * P:(k + 1) * P],
                                          V_all[:, bass.ds(p, 1), k, h * HD:(h + 1) * HD].rearrange("t o d -> t (o d)"),
                                          start=(k == 0), stop=(k == NT - 1))
                            last.then_inc(g_pe, 1)
                pe.wait_ge(s_late_first, 2 * 16)
                turn_a(0, 0, bank[7])
                project(0, 0)
                turn_x(0, 0, bank[7])
                pe.wait_ge(s_late, 5 * 16)
                for e in range(2):
                    up(0, 0, e)

            def route(c, q):
                pe.wait_ge(c_xnTk, c + 1)
                pe.wait_ge(c_y, c + 1)
                for t in range(CT):
                    last = mm(bank[7][:, t * E:(t + 1) * E], xnT[q][:, t * P:(t + 1) * P], Wr_sb[:, :], start=True, stop=True)
                last.then_inc(c_lg, 1)

            def down(c, e):
                pe.wait_ge(e_hid, c * NE + (e + 3))
                if e == 0:
                    pe.wait_ge(c_shared, c + 1)
                elif e >= 2:
                    pe.wait_ge(e_part, c * E + (e - 1))
                for t in range(CT):
                    last = mm(bank[4 + e % 2][:, t * P:(t + 1) * P], hid[e % 3][:, t * P:(t + 1) * P], dn_sb[:, e, :], start=True, stop=True)
                last.then_inc(e_dn, 1)

            def down_shared(c):
                pe.wait_ge(e_hid, c * NE + (NE + 2))
                pe.wait_ge(e_part, c * E + (E - 1))
                for t in range(CT):
                    mm(bank[4][:, t * P:(t + 1) * P], hid[E % 3][:, t * P:(t + 1) * P], dn_sb[:, E, :], start=True, stop=False)
                    last = mm(bank[4][:, t * P:(t + 1) * P], hid[(E + 1) % 3][:, t * P:(t + 1) * P], dn_sb[:, E + 1, :], start=False, stop=True)
                last.then_inc(e_dn, 1)

            def step(c, b, q, last, started=0):
                if not started:
                    up(c, q, 0)
                for e in range(1, NE):
                    if e >= started:
                        up(c, q, e)
                    if not last and e == 3:
                        pe.wait_ge(c_lgk, c + 1)
                        project(c + 1, 1 - q)
                    if e < E:
                        down(c, e - 1)
                    if e == NE - 1:
                        down(c, E - 1)
                        if not last:
                            route(c + 1, 1 - q)
                    if not last:
                        if e == 1:
                            pe.wait_ge(c_xnTk, c + 1)
                            turn_a(c + 1, 1 - q)
                        if e == 7:
                            turn_x(c + 1, 1 - q)
                down_shared(c)

            pe.wait_ge(attn_done, 1)
            route(0, 0)
            step(0, 0, 0, False, started=2)
            with pe.Fori(0, NCH // 2 - 1) as i:
                step(i * 2 + 1, i, 1, False)
                step(i * 2 + 2, i + 1, 0, False)
            step(NCH - 1, NCH // 2 - 1, 1, True)

        @block.vector
        def _(dve):
            tt, ts = nc.vector.tensor_tensor, nc.vector.tensor_scalar
            dve.wait_ge(s_wkv, 80)
            tt(Wkv_sb[:, 2, :], Wkv_sb[:, 0, :], Wkv_sb[:, 1, :], ALU.add).then_inc(wkv_added, 1)
            for u in range(1):
                nc.vector.memzero(sv[64:P, u].rearrange("r k h v s -> r (k h v s)").bitcast(F32)).then_inc(pad_zeroed, 1)
            nc.vector.memset(Vring[:, :, :, :, :], 0.0).then_inc(prep_chain, 1)
            nc.vector.memset(test[:, 0:1], 1.0).then_inc(prep_chain, 1)
            dve.wait_ge(s_pack, 16)
            nc.vector.tensor_copy(head_sum_h[:, :], head_sum).then_inc(norm_maxed, 1)
            dve.wait_ge(prep_chain, 1)
            nc.vector.memset(Vring[:, :, :, :, HD:HD + 1], 1.0).then_inc(prep_chain, 1)
            links = [3]

            def link(ins):
                links[0] += 1
                ins.then_inc(prep_chain, 1)
                dve.wait_ge(prep_chain, links[0])

            for b in range(B):
                for h in range(2):
                    dve.wait_ge(v_ready, 2 * b + h + 1)
                    nc.vector.tensor_copy(V_all[:, b * PPB:(b + 1) * PPB, CT * h:CT * (h + 1), :].rearrange("p w t e -> p t w e"),
                                          bank[7].rearrange("p (t w e) -> p t w e", t=CT, w=PPB)).then_inc(v_kept, 1)
                    dve.wait_ge(norm_ready, 2 * b + h + 1)
                    nc.vector.reduce_max(nmax[:, 2 * b + h:2 * b + h + 1], bank[6][0:64, :], AX_X).then_inc(norm_maxed, 1)
                if b < 3:
                    n, v, t0 = ((0, 0, 0), (0, 1, 0), (1, 1, K_SHARE))[b]
                    dve.wait_ge(qk_kept, 4)
                    dve.wait_ge(s_rows, 32)
                    hi, mid, lo = (stage[:, n, a, v * S + t0:(v + 1) * S] for a in range(NPART))
                    f, r = probs[:, 4, t0:S], probs[:, 5, t0:S]
                    link(tt(f, qkT[n][:, t0:S], rows_sb[:, v ^ n, t0:S], ALU.mult))
                    link(nc.vector.tensor_copy(hi, f))
                    link(tt(r, f, hi, ALU.subtract))
                    link(nc.vector.tensor_copy(mid, r))
                    link(tt(lo, r, mid, ALU.subtract))
                    dve.sem_inc(stage_k_rest if n else stage_ready[0], 1)

            dve.wait_ge(norm_maxed, 2 * B + 1)
            link(nc.vector.reduce_max(testv[0:64, 0:1], nmax[:, :], AX_X))
            link(nc.vector.tensor_copy(testv[0:32, 1:2], testv[32:64, 0:1]))
            link(tt(testv[0:32, 2:3], testv[0:32, 0:1], testv[0:32, 1:2], ALU.mult))
            link(ts(test[0:32, 0:1], testv[0:32, 2:3], NORM_LIMIT, None, ALU.is_le))
            dve.wait_ge(v_squared, 2 * B)
            dve.wait_ge(qk_kept, 4 * B)
            link(ts(testv[:, :], sums[:, :], SUM_LIMIT, None, ALU.is_le))
            link(nc.vector.tensor_reduce(test[:, 1:2], testv[:, :], AX_X, ALU.min))
            tt(test[:, 2:3], test[:, 0:1], test[:, 1:2], ALU.mult).then_inc(test_ready, 1)
            dve.wait_ge(test_summed, 1)
            nc.vector.tensor_copy(flag[0:1, 0:1], bank[0][0:1, 0:1]).then_inc(flag_ready, 1)
            dve.wait_ge(flag_ready, 1)
            fits = dve.value_load(flag[0:1, 0:1], min_val=0, max_val=P)

            ln = Chain(dve, ln_chain, 2)
            ln2 = Chain(dve, ln2_chain, 2)
            rt = Chain(dve, route_chain, 8)

            def statistics(chain, src, st, m, v, s):
                for t in range(CT):
                    last = nc.vector.bn_stats(st[:, t, :], src[:, t * P:(t + 1) * P])
                chain.link(last)
                apart(dve)
                for t in range(CT):
                    last = nc.vector.bn_aggr(m[:, t, :], st[:, t, :])
                chain.link(last)
                ts(v, m[:, :, 1], EPS, None, ALU.add).then_inc(s, 1)

            def normal_rows(dst, src, m, r):
                for t in range(CT):
                    last = ts(dst[:, t * P:(t + 1) * P], src[:, t * P:(t + 1) * P], m[:, t, 0:1], r[:, t:t + 1], ALU.subtract, ALU.mult)
                return last

            def ln1_statistics(c, i, q):
                ln.start(c)
                dve.wait_ge(c_x[q], i * 16 + 16)
                dve.wait_ge(c_wo, c + 1)
                tt(y_pre[q], bank[7], x_res[q], ALU.add).then_inc(c_y, 1)
                dve.wait_ge(c_y, c + 1)
                statistics(ln, y_pre[q], stats, mv, var, c_var)

            def ln1_rows(c, q):
                dve.wait_ge(c_rstd, c + 1)
                normal_rows(xn[q], y_pre[q], mv, rstd).then_inc(c_xn, 1)

            dve.sem_inc(c_shared, 1)
            dve.sem_inc(e_hid, 2)
            with dve.If(fits >= P):
                def copy_v(i, p):
                    nc.vector.tensor_copy(Vring[:, p % 3, :, :, 0:HD],
                                          V_all[:, bass.ds(i * BODY_PAIRS + p, 1), :, :].rearrange("r o t (h d) -> r (o t) h d", h=2)).then_inc(v_copied, 1)

                def fix_diagonal(i, m):
                    kt = (m % TPP) // 2
                    dve.wait_ge(scores_ready, i * TPB + (m + 1))
                    d = slot[m % 3][:, kt * P:(kt + 1) * P]
                    tt(d, d, diag_fix, ALU.mult).then_inc(diag_done, 1)

                def evacuate(i, p):
                    dve.wait_ge(prob_slots_free, (i * BODY_PAIRS + (p + 1)) * NT + FREE0)
                    nc.vector.tensor_copy(osb[:, :], bank[6]).then_inc(o_evacuated, 1)

                def normalise(i, p):
                    dve.wait_ge(o_turned, i * BODY_PAIRS + (p + 1))
                    o = bank[7].rearrange("t (c g r) -> t g c r", c=CT, g=4)
                    rv = rec[:, :].rearrange("t (g c) -> t g c", g=4)
                    nc.vector.reciprocal(rv, o[:, :, :, HD]).then_inc(rec_done, 1)
                    dve.wait_ge(rec_done, i * BODY_PAIRS + (p + 1))
                    tt(attn_pair[:, bass.ds(i * BODY_PAIRS + p, 1), :, :, :].rearrange("t o g c d -> t (o g c) d"),
                       o[:, :, :, 0:HD].rearrange("t g c d -> t g c d"),
                       rv.unsqueeze(3).to_broadcast([P, 4, CT, HD]), ALU.mult).then_inc(o_kept, 1)

                def tile_step(i, m, final=False):
                    r, p = m % TPP, m // TPP
                    if r == 3:
                        evacuate(i, p - 1)
                    fix_diagonal(i, m)
                    if r == 6:
                        normalise(i, p - 1)
                    if r == 10 and not (final and p == PAIRS - 1):
                        copy_v(i, p + 1)

                dve.sem_inc(score_slots_free, FREE0)
                dve.sem_inc(prob_slots_free, FREE0)
                copy_v(0, 0)
                for m in range(7):
                    fix_diagonal(0, m)
                with dve.Fori(0, ROUNDS) as i:
                    for m in range(7, TPB + 7):
                        tile_step(i, m)
                for m in range(TAIL * TPP + 7, TILES):
                    tile_step(0, m, final=True)
                    if m == TILES - TPP + 3:
                        ln1_statistics(0, 0, 0)
                    if m == TILES - TPP + 8:
                        ln1_rows(0, 0)
                evacuate(0, PAIRS - 1)
                normalise(0, PAIRS - 1)
                dve.wait_ge(o_kept, PAIRS)
                dve.sem_inc(attn_done, 1)
            with dve.Else():
                dve.wait_ge(g_band_in, 16)
                dve.sem_inc(g_dve, 1)
                chain = Chain(dve, g_dve, G_LINKS)
                with dve.Fori(0, PAIRS) as p:
                    dve.wait_ge(g_loaded, p * 32 + 32)
                    apart(dve)
                    for h in range(2):
                        with dve.Fori(0, NT) as t:
                            n = p * 16 + h * 8 + t
                            chain.start(n, 1)
                            chain.link(nc.vector.tensor_copy(g_q, g_qk[:, 0, h, bass.ds(t * P, P)]))
                            dve.wait_ge(g_pe, n * 3 + 1)
                            chain.link(ts(g_scores, slot[0], SCALE, -CLAMP, ALU.mult, ALU.max))
                            chain.link(ts(g_scores, g_scores, CLAMP, None, ALU.min))
                            chain.link(tt(g_scores, g_scores, g_band[:, bass.ds(t * -P + (S - P), S)], ALU.mult))
                            chain.link(ts(g_scores, g_scores, -CLAMP, CLAMP, ALU.max, ALU.min))
                            chain.link(nc.vector.tensor_reduce(g_stat[:, 0:1], g_scores, AX_X, ALU.max, negate=True))
                            dve.wait_ge(g_act, n + 1)
                            dve.wait_ge(g_pe, n * 3 + 2)
                            chain.link(nc.vector.tensor_copy(g_pT, slot[1]))
                            chain.link(nc.vector.reciprocal(g_stat[:, 2:3], g_stat[:, 1:2]))
                            dve.wait_ge(g_pe, n * 3 + 3)
                            chain.link(ts(xT[:, bass.ds(p * P + (h * 64) + t * HD, HD)], bank[4][:, 0:HD], g_stat[:, 2:3], None, ALU.mult))
                            chain.end()
                dve.sem_inc(attn_done, 1)
                ln1_statistics(0, 0, 0)
                ln1_rows(0, 0)

            def route(c, q):
                rt.start(c)
                dve.wait_ge(c_lg, c + 1)
                nc.vector.tensor_copy(logits, bank[7][:, 0:CT * E].rearrange("t (c e) -> t c e", c=CT)).then_inc(c_lgk, 1)
                dve.wait_ge(c_lgk, c + 1)
                apart(dve)
                for t in range(CT):
                    last = nc.vector.max(top8[:, t, :], logits[:, t, :])
                rt.link(last)
                tt(gap, top8[:, :, 1], top8[:, :, 0], ALU.subtract).then_inc(c_gap, 1)
                for t in range(CT):
                    last = nc.vector.max_index(top_i[:, t, :], top8[:, t, :], logits[:, t, :])
                rt.link(last)
                rt.link(nc.vector.tensor_copy(idx_f, top_i))
                lanes = lane8.rearrange("t (c e) -> t c e", c=CT)
                tt(eq1, lanes, idx_f[:, :, 0:1].to_broadcast([P, CT, E]), ALU.is_equal)
                tt(eq2, lanes, idx_f[:, :, 1:2].to_broadcast([P, CT, E]), ALU.is_equal)
                dve.wait_ge(c_exp, c + 1)
                rt.link(ts(w2, gexp, 1.0, None, ALU.add))
                rt.link(nc.vector.reciprocal(w1, w2))
                rt.link(tt(w2, gexp, w1, ALU.mult))
                tt(eq1, eq1, w1.unsqueeze(2).to_broadcast([P, CT, E]), ALU.mult)
                rt.link(tt(eq2, eq2, w2.unsqueeze(2).to_broadcast([P, CT, E]), ALU.mult))
                rt.link(tt(weights[q], eq1, eq2, ALU.add))
                rt.end()

            def hidden(c, e):
                dve.wait_ge(e_silu, c * NE + (e + 1))
                tt(hid[e % 3], silu[e % 2], bank[2 + e % 2], ALU.mult).then_inc(e_hid, 1)

            def weigh(c, q, e):
                dve.wait_ge(e_dn, c * (E + 1) + (e + 1))
                if e >= 2:
                    dve.wait_ge(e_acc, c * E + (e - 1))
                tt(part_e[e % 2].rearrange("t (c d) -> t c d", c=CT), bank[4 + e % 2].rearrange("t (c d) -> t c d", c=CT),
                   weights[q][:, :, e:e + 1].to_broadcast([P, CT, P]), ALU.mult).then_inc(e_part, 1)

            def step(c, i, q, last, previous=True):
                for e in range(NE):
                    hidden(c, e)
                    if e == 1 and not previous:
                        route(c, q)
                    if e == 1 and previous:
                        ln2_statistics(c - 1, 1 - q)
                    if 1 <= e <= E - 1:
                        weigh(c, q, e - 1)
                    if e == 3 and previous:
                        ln2_rows(c - 1, 1 - q)
                    if e == 4 and not last:
                        ln1_statistics(c + 1, i + q, 1 - q)
                    if e == 5 and not last:
                        ln1_rows(c + 1, 1 - q)
                weigh(c, q, E - 1)
                if not last:
                    route(c + 1, 1 - q)
                dve.wait_ge(e_dn, c * (E + 1) + (E + 1))
                dve.wait_ge(e_acc, c * E + E)
                dve.wait_ge(c_store[q], i * 16 + 16)
                tt(outb[q], bank[4], acc[q], ALU.add).then_inc(c_shared, 1)

            def ln2_statistics(c, q):
                ln2.start(c)
                dve.wait_ge(c_shared, c + 2)
                statistics(ln2, outb[q], stats2, mv2, var2, c_var2)

            def ln2_rows(c, q):
                dve.wait_ge(c_rstd2, c + 1)
                normal_rows(outb[q], outb[q], mv2, rstd2).then_inc(c_out, 1)

            step(0, 0, 0, False, previous=False)
            with dve.Fori(0, NCH // 2 - 1) as i:
                step(i * 2 + 1, i, 1, False)
                step(i * 2 + 2, i + 1, 0, False)
            step(NCH - 1, NCH // 2 - 1, 1, True)
            ln2_statistics(NCH - 1, 1)
            ln2_rows(NCH - 1, 1)


_INS = ["L0_attn_x", "L0_attn_Wq", "L0_attn_Wk", "L0_attn_Wv", "L0_attn_Wo", "L0_attn_W_down_kv", "L0_attn_W_up_k",
        "L0_attn_W_up_v", "L0_ffn_w_router", "L0_ffn_fc1_w", "L0_ffn_fc2_w", "L0_ffn_gate_w", "L0_ffn_up_w", "L0_ffn_down_w"]


def kernel(**inputs):
    import concourse.bacc as _bacc
    from concourse.bass_utils import run_bass_kernel_spmd as _run

    nc = _bacc.Bacc("TRN2", target_bir_lowering=False, num_devices=1)
    shape = inputs["L0_attn_x"].shape
    consts = dict(zip(("decay_rows", "const_pack", "decay_band"), shape_constants(shape[1], shape[2])))
    arrays, args = {}, []
    for name, a in [(n, inputs[n]) for n in _INS] + list(consts.items()):
        a = np.ascontiguousarray(a)
        arrays[f"in_{name}"] = a
        args.append(nc.dram_tensor(f"in_{name}", a.shape, mybir.dt.from_np(a.dtype), kind="ExternalInput").ap())
    out = nc.dram_tensor("out_0", shape, F32, kind="ExternalOutput").ap()
    block_kernel(nc, *args, out)
    r = _run(nc, [arrays], core_ids=[0])
    return r.results[0]["out_0"]
```
